# Optimizing a Trainium2 kernel written in Bass

```python
import numpy as np
import jax
import jax.numpy as jnp

def _softmax(x, axis=-1):
    return jax.nn.softmax(x, axis=axis)

def _gelu(x):
    return jax.nn.gelu(x, approximate=True)

def _silu(x):
    return jax.nn.silu(x)

def _sigmoid(x):
    return jax.nn.sigmoid(x)

def _layernorm(x, axis=-1, eps=1e-05):
    m = jnp.mean(x, axis=axis, keepdims=True)
    v = jnp.var(x, axis=axis, keepdims=True)
    return (x - m) / jnp.sqrt(v + eps)

def _scatter_add(tgt, idx, src, axis=0):
    return tgt.at[idx].add(src)

def _segment_sum(src, seg, n):
    return jax.ops.segment_sum(src, seg, n)
kernel_name = 'mk_conv_preact_d2_conv_nchw256_r2_2fc7af'

def setup_inputs(seed: int=0):
    np.random.seed(seed)
    _w = jnp.asarray

    def _rec_inputs():
        import jax
        import jax.numpy as jnp
        _gk = jax.random.key(seed)
        x = 1.648e-05 + 1 * jax.random.normal(jax.random.fold_in(_gk, 1), (4, 128, 48, 48), jnp.float32)
        return x
    x = _rec_inputs()

    def _L0_conv_setup():
        import jax, jax.numpy as jnp
        import numpy as np
        from jax import lax
        B, CHI, CHO, H, W = (4, 128, 128, 48, 48)
        K = 9
        BN_EPS = 1e-05

        def _bilinear_gather(img, py, px):
            Hin, Win = (img.shape[1], img.shape[2])
            y0 = jnp.floor(py)
            x0 = jnp.floor(px)
            ly = py - y0
            lx = px - x0
            y0i = y0.astype(jnp.int32)
            x0i = x0.astype(jnp.int32)

            def corner(yi, xi, wgt):
                valid = (yi >= 0) & (yi < Hin) & (xi >= 0) & (xi < Win)
                yc = jnp.clip(yi, 0, Hin - 1)
                xc = jnp.clip(xi, 0, Win - 1)
                v = img[:, yc, xc]
                return v * (wgt * valid.astype(wgt.dtype))[None]
            return corner(y0i, x0i, (1 - ly) * (1 - lx)) + corner(y0i, x0i + 1, (1 - ly) * lx) + corner(y0i + 1, x0i, ly * (1 - lx)) + corner(y0i + 1, x0i + 1, ly * lx)

        def _forward(x, w_offset, b_offset, w_conv, b_conv, gamma, beta):
            om = lax.conv_general_dilated(x, w_offset, window_strides=(1, 1), padding=((1, 1), (1, 1)), dimension_numbers=('NCHW', 'OIHW', 'NCHW'))
            om = om + b_offset[None, :, None, None]
            dy = om[:, 0:2 * K:2]
            dx = om[:, 1:2 * K:2]
            mask = jax.nn.sigmoid(om[:, 2 * K:])
            ky, kx = jnp.meshgrid(jnp.arange(3), jnp.arange(3), indexing='ij')
            ky = ky.reshape(K).astype(x.dtype)
            kx = kx.reshape(K).astype(x.dtype)
            hh = jnp.arange(x.shape[2], dtype=x.dtype)
            ww = jnp.arange(x.shape[3], dtype=x.dtype)
            py = dy + (hh[None, :, None] + ky[:, None, None] - 1.0)[None]
            px = dx + (ww[None, None, :] + kx[:, None, None] - 1.0)[None]
            cols = jax.vmap(_bilinear_gather)(x, py, px)
            cols = cols * mask[:, None]
            wk = w_conv.reshape(w_conv.shape[0], w_conv.shape[1], K)
            out = jnp.einsum('bckhw,ock->bohw', cols, wk) + b_conv[None, :, None, None]
            mu = out.mean(axis=(0, 2, 3))
            var = out.var(axis=(0, 2, 3))
            xh = (out - mu[None, :, None, None]) * lax.rsqrt(var + BN_EPS)[None, :, None, None]
            y = gamma[None, :, None, None] * xh + beta[None, :, None, None]
            return jax.nn.relu(y)
        key = jax.random.key(seed)
        k1, k2, k3 = jax.random.split(key, 3)
        x = jax.random.normal(k1, (B, CHI, H, W), dtype=jnp.float32)
        w_offset = jax.random.normal(k2, (3 * K, CHI, 3, 3), dtype=jnp.float32) * 0.01
        b_offset = jnp.zeros((3 * K,), dtype=jnp.float32)
        fan_in = CHI * K
        w_conv = jax.random.normal(k3, (CHO, CHI, 3, 3), dtype=jnp.float32) / np.sqrt(fan_in)
        b_conv = jnp.zeros((CHO,), dtype=jnp.float32)
        gamma = jnp.ones((CHO,), dtype=jnp.float32)
        beta = jnp.zeros((CHO,), dtype=jnp.float32)
        return {'x': x, 'w_offset': w_offset, 'b_offset': b_offset, 'w_conv': w_conv, 'b_conv': b_conv, 'gamma': gamma, 'beta': beta}
    _L0_conv_all = _L0_conv_setup()
    _L0_conv_in = {k: v for k, v in _L0_conv_all.items() if k in ('w_offset', 'b_offset', 'w_conv', 'b_conv', 'gamma', 'beta')}
    del _L0_conv_all

    def _L1_conv_setup():
        import jax, jax.numpy as jnp
        import numpy as np
        STRIDE = (1, 1)
        PADDING = ((1, 1), (1, 1))
        DILATION = (1, 1)
        GROUPS = 1
        key = jax.random.key(seed)
        k1, k2, k3 = jax.random.split(key, 3)
        N, C_in, H, W = (32, 128, 32, 32)
        C_out, kH, kW = (128, 3, 3)
        x = jax.random.normal(k1, (N, C_in, H, W), dtype=jnp.float32)
        fan_in = C_in * kH * kW
        weight = jax.random.normal(k2, (C_out, C_in, kH, kW), dtype=jnp.float32) / np.sqrt(fan_in)
        bias = jax.random.normal(k3, (C_out,), dtype=jnp.float32) * 0.01
        return {'x': x, 'weight': weight, 'bias': bias}
    _L1_conv_all = _L1_conv_setup()
    _L1_conv_in = {k: v for k, v in _L1_conv_all.items() if k in ('weight', 'bias')}
    del _L1_conv_all
    return {'x': x, 'L0_conv_w_offset': _L0_conv_in['w_offset'], 'L0_conv_b_offset': _L0_conv_in['b_offset'], 'L0_conv_w_conv': _L0_conv_in['w_conv'], 'L0_conv_b_conv': _L0_conv_in['b_conv'], 'L0_conv_gamma': _L0_conv_in['gamma'], 'L0_conv_beta': _L0_conv_in['beta'], 'L1_conv_weight': _L1_conv_in['weight'], 'L1_conv_bias': _L1_conv_in['bias']}

def reference(x, L0_conv_w_offset, L0_conv_b_offset, L0_conv_w_conv, L0_conv_b_conv, L0_conv_gamma, L0_conv_beta, L1_conv_weight, L1_conv_bias):
    import jax
    import jax.numpy as jnp

    def _L0_conv_ref(x, w_offset, b_offset, w_conv, b_conv, gamma, beta):
        import jax, jax.numpy as jnp
        import numpy as np
        from jax import lax
        B, CHI, CHO, H, W = (4, 128, 128, 48, 48)
        K = 9
        BN_EPS = 1e-05

        def _bilinear_gather(img, py, px):
            Hin, Win = (img.shape[1], img.shape[2])
            y0 = jnp.floor(py)
            x0 = jnp.floor(px)
            ly = py - y0
            lx = px - x0
            y0i = y0.astype(jnp.int32)
            x0i = x0.astype(jnp.int32)

            def corner(yi, xi, wgt):
                valid = (yi >= 0) & (yi < Hin) & (xi >= 0) & (xi < Win)
                yc = jnp.clip(yi, 0, Hin - 1)
                xc = jnp.clip(xi, 0, Win - 1)
                v = img[:, yc, xc]
                return v * (wgt * valid.astype(wgt.dtype))[None]
            return corner(y0i, x0i, (1 - ly) * (1 - lx)) + corner(y0i, x0i + 1, (1 - ly) * lx) + corner(y0i + 1, x0i, ly * (1 - lx)) + corner(y0i + 1, x0i + 1, ly * lx)

        def _forward(x, w_offset, b_offset, w_conv, b_conv, gamma, beta):
            om = lax.conv_general_dilated(x, w_offset, window_strides=(1, 1), padding=((1, 1), (1, 1)), dimension_numbers=('NCHW', 'OIHW', 'NCHW'))
            om = om + b_offset[None, :, None, None]
            dy = om[:, 0:2 * K:2]
            dx = om[:, 1:2 * K:2]
            mask = jax.nn.sigmoid(om[:, 2 * K:])
            ky, kx = jnp.meshgrid(jnp.arange(3), jnp.arange(3), indexing='ij')
            ky = ky.reshape(K).astype(x.dtype)
            kx = kx.reshape(K).astype(x.dtype)
            hh = jnp.arange(x.shape[2], dtype=x.dtype)
            ww = jnp.arange(x.shape[3], dtype=x.dtype)
            py = dy + (hh[None, :, None] + ky[:, None, None] - 1.0)[None]
            px = dx + (ww[None, None, :] + kx[:, None, None] - 1.0)[None]
            cols = jax.vmap(_bilinear_gather)(x, py, px)
            cols = cols * mask[:, None]
            wk = w_conv.reshape(w_conv.shape[0], w_conv.shape[1], K)
            out = jnp.einsum('bckhw,ock->bohw', cols, wk) + b_conv[None, :, None, None]
            mu = out.mean(axis=(0, 2, 3))
            var = out.var(axis=(0, 2, 3))
            xh = (out - mu[None, :, None, None]) * lax.rsqrt(var + BN_EPS)[None, :, None, None]
            y = gamma[None, :, None, None] * xh + beta[None, :, None, None]
            return jax.nn.relu(y)
        return _forward(x, w_offset, b_offset, w_conv, b_conv, gamma, beta)

    def _L1_conv_ref(x, weight, bias):
        import jax, jax.numpy as jnp
        import numpy as np
        STRIDE = (1, 1)
        PADDING = ((1, 1), (1, 1))
        DILATION = (1, 1)
        GROUPS = 1
        y = jax.lax.conv_general_dilated(x, weight, window_strides=STRIDE, padding=PADDING, rhs_dilation=DILATION, dimension_numbers=('NCHW', 'OIHW', 'NCHW'), feature_group_count=GROUPS)
        return y + bias[None, :, None, None]

    def _gn(v, G=32, eps=1e-05):
        B_, C_, H_, W_ = v.shape
        g = v.reshape(B_, G, C_ // G, H_, W_)
        m = jnp.mean(g, axis=(2, 3, 4), keepdims=True)
        s = jnp.var(g, axis=(2, 3, 4), keepdims=True)
        return ((g - m) / jnp.sqrt(s + eps)).reshape(v.shape)

    def _ln_c(v, eps=1e-06):
        m = jnp.mean(v, axis=1, keepdims=True)
        s = jnp.var(v, axis=1, keepdims=True)
        return (v - m) / jnp.sqrt(s + eps)

    def _ln_t(v, eps=1e-05):
        m = jnp.mean(v, axis=-1, keepdims=True)
        s = jnp.var(v, axis=-1, keepdims=True)
        return (v - m) / jnp.sqrt(s + eps)

    def _to_tokens(v):
        B_, C_, H_, W_ = v.shape
        return v.reshape(B_, C_, H_ * W_).transpose(0, 2, 1)

    def _from_tokens(t, like):
        B_, C_, H_, W_ = like.shape
        return t.transpose(0, 2, 1).reshape(B_, C_, H_, W_)
    x = x + _L0_conv_ref(_gn(x), L0_conv_w_offset, L0_conv_b_offset, L0_conv_w_conv, L0_conv_b_conv, L0_conv_gamma, L0_conv_beta)
    x = x + _L1_conv_ref(_gn(x), L1_conv_weight, L1_conv_bias)
    return x

_drawn_inputs = setup_inputs


def setup_inputs(seed=0):
    import zlib

    import numpy as np

    out = dict(_drawn_inputs(seed))
    spreads = {'L0_conv_b_offset': (0.0, 0.1),
     'L0_conv_b_conv': (0.0, 0.8),
     'L0_conv_gamma': (1.0, 0.2),
     'L0_conv_beta': (0.0, 0.1)}
    factors = {'L1_conv_bias': 8.0}
    for name, (base, spread) in spreads.items():
        noise = np.random.default_rng([zlib.crc32(name.encode()), seed]).standard_normal(out[name].shape)
        drawn = base * np.exp(spread * noise) if base else spread * noise
        out[name] = jnp.asarray(drawn.astype(out[name].dtype))
    for name, factor in factors.items():
        out[name] = (out[name] * factor).astype(out[name].dtype)
    return out
```

```python
import concourse.bass as bass
from concourse import mybir
from contextlib import ExitStack

F32 = mybir.dt.float32
I32 = mybir.dt.int32
ALU = mybir.AluOpType
ACT = mybir.ActivationFunctionType

P = 128
B, H, W = 4, 48, 48
HW = H * W
TAPS = 9
PW = W + 2
TILES = 3
CP = TILES * P
ROWS = CP // W
CHUNKS = HW // CP
PAIRS = CHUNKS // 2
ALL = B * CHUNKS
GROUP = 4
EPS = 1e-5
TT = 20
TG = 4
LEAD = 64
TABLE = LEAD + TT * P
ROUND = 12582912.0
NEWTON = 3
RSTEPS = 3 + 3 * NEWTON
LERPS = 3 * TILES


def build(nc, x_d, woff_d, wconv_d, w1_d, boff_d, par_d, grid_d, out_d):
    tables = [nc.dram_tensor(f"corner_table{b}", [TABLE, 4 * P], F32, kind="Internal").ap() for b in range(B)]

    with ExitStack() as ctx:
        def sb(name, shape, dt=F32):
            return ctx.enter_context(nc.sbuf_tensor(name, shape, dt))

        def ps(name):
            return ctx.enter_context(nc.psum_tensor(name, [P, 512], F32))

        def sem(name):
            return ctx.enter_context(nc.semaphore(name))

        x = sb("x", [P, B * HW])
        o = sb("o", [P, B * HW])
        xn = sb("xn", [P, B * PW, PW])
        xt = sb("xt", [P, 52 * PW])
        tok = sb("tok", [P, TT, P])
        g = sb("g", [P, TAPS, TILES, 4, P])
        acc = sb("acc", [P, 3, TILES, P])
        cols = sb("cols", [P, 2, CP])
        woff = sb("woff", [P, TAPS, 27])
        wconv = sb("wconv", [P, TAPS, P])
        w1 = tok[:, 0:TAPS, :]
        boff = sb("boff", [27, 1])
        par = sb("par", [P, 5])
        grid = sb("grid", [P, CHUNKS, TILES, 18])
        ident = sb("ident", [P, P])
        gavg = sb("gavg", [P, P])
        om = sb("om", [27, CP])
        mask = sb("mask", [P, TILES, 9])
        pos = sb("pos", [P, TILES, 18])
        low = sb("low", [P, TILES, 18])
        frac = sb("frac", [P, TILES, 18])
        rest = sb("rest", [P, TILES, 18])
        my = sb("my", [P, 2, TILES, 9])
        idxf = sb("idxf", [P, TILES, 9])
        idx = sb("idx", [P, 2, TILES, 9], I32)
        wt = sb("wt", [P, 2, 4, TILES, 9])
        bst = sb("bst", [P, CHUNKS, 6])
        mv = sb("mv", [P, 2])
        dev = sb("dev", [P, 2])
        gn = sb("gn", [P, 2])
        ost = sb("ost", [P, ALL, 6])
        omv = sb("omv", [P, 2])
        rq = sb("rq", [P, 3])
        bna = sb("bna", [P, 4])

        OM, OT, TP0, TP1, CO0, CO1, PT0, PT1 = (ps(n) for n in ("OM", "OT", "TP0", "TP1", "CO0", "CO1", "PT0", "PT1"))
        TP, CO, PT = (TP0, TP1), (CO0, CO1), (PT0, PT1)
        ST = OT[:, 500:502]

        x0_in, xr_in, wo_in, wc_in, w1_in, gr_in = (sem(n) for n in ("x0_in", "xr_in", "wo_in", "wc_in", "w1_in", "gr_in"))
        consts = sem("consts")
        st = sem("st")
        gm_done = sem("gm_done")
        gn_ready = sem("gn_ready")
        mvr = sem("mvr")
        xt_ready = sem("xt_ready")
        xn_ready = sem("xn_ready")
        tok_turned = sem("tok_turned")
        tok_ready = sem("tok_ready")
        ends = sem("ends")
        tabled = sem("tabled")
        om_ready = sem("om_ready")
        om_copied = sem("om_copied")
        om_turned = sem("om_turned")
        mask_ready = sem("mask_ready")
        idx_ready = sem("idx_ready")
        gathered = [sem(f"gathered{k}") for k in range(TAPS)]
        scaled = sem("scaled")
        lerped = sem("lerped")
        turned = sem("turned")
        copied = sem("copied")
        conved = sem("conved")
        out_copied = sem("out_copied")
        granted = sem("granted")
        passed = sem("passed")
        ix = sem("ix")
        rs = sem("rs")
        ostat = sem("ostat")
        bn_ready = sem("bn_ready")
        relued = sem("relued")
        summed = sem("summed")
        normed = sem("normed")
        conv1 = sem("conv1")
        fin = sem("fin")
        stored = sem("stored")

        block = ctx.enter_context(nc.Block())

        def interior(t, row, rows):
            return t[:, bass.ds(row, rows), 1:1 + W]

        def rows_of(t, start, n):
            return t[:, bass.ds(start, n)].rearrange("p (r w) -> p r w", w=W)

        def alone(eng):
            eng.sem_inc(passed, 1)

        @block.sync
        def _(sp):
            sp.sem_inc(scaled, TAPS * TILES)
            sp.sem_inc(lerped, TAPS * LERPS)
            sp.sem_inc(turned, TAPS)
            sp.sem_inc(copied, TAPS)
            sp.sem_inc(conved, TAPS)
            sp.sem_inc(out_copied, 2)
            sp.sem_inc(fin, 2)
            sp.sem_inc(granted, 1)
            sp.dma_start(x[:, 0:HW], x_d[:, 0]).then_inc(x0_in, 16)
            sp.dma_start(woff[:], woff_d).then_inc(wo_in, 16)
            sp.dma_start(boff[:], boff_d).then_inc(wo_in, 16)
            sp.dma_start(grid[:], grid_d).then_inc(gr_in, 16)
            sp.dma_start(x[:, HW:].rearrange("p (b n) -> p b n", b=B - 1), x_d[:, 1:B]).then_inc(xr_in, 16)
            sp.dma_start(wconv[:], wconv_d).then_inc(wc_in, 16)
            sp.dma_start(par[:], par_d).then_inc(wc_in, 16)
            sp.wait_ge(consts, 1)
            zeros = acc[0:LEAD].rearrange("p a t c -> p (a t c)")[:, 0:4 * P]
            for b in range(B):
                sp.dma_start(tables[b][0:LEAD], zeros).then_inc(ends, 16)
                sp.dma_start(tables[b][TABLE - LEAD:TABLE], zeros).then_inc(ends, 16)
            sp.wait_ge(ends, 2 * B * 16)
            for b in range(B):
                for j in range(TT // TG):
                    sp.wait_ge(tok_ready, b * (TT // TG) + (j + 1))
                    for q in range(4):
                        shift = PW * (q // 2) + q % 2
                        row = LEAD + j * TG * P - shift
                        dst = tables[b][row:row + TG * P, q * P:(q + 1) * P]
                        sp.dma_start(dst.rearrange("(t p) c -> p t c", p=P), tok[:, j * TG:(j + 1) * TG, :]).then_inc(tabled, 16)
            sp.wait_ge(tabled, B * 16 * TT)
            sp.dma_start(w1, w1_d).then_inc(w1_in, 16)
            with sp.Fori(0, B * PAIRS) as i:
                sp.wait_ge(fin, 2 * i + 4)
                sp.dma_start(out_d[:, bass.ds(i * (2 * CP), 2 * CP)], x[:, bass.ds(i * (2 * CP), 2 * CP)]).then_inc(stored, 16)
            sp.wait_ge(stored, 16 * B * PAIRS)

        @block.gpsimd
        def _(pl):
            pl.memset(acc[:], 0.0).then_inc(consts, 1)
            pl.memset(ident[:], 0.0).then_inc(consts, 1)
            pl.memset(gavg[:], 1.0 / GROUP).then_inc(consts, 1)
            pl.wait_ge(consts, 3)
            pl.affine_select(out=ident[:], in_=ident[:], compare_op=ALU.not_equal, fill=1.0, base=0,
                             pattern=[[-1, P]], channel_multiplier=1).then_inc(consts, 1)
            gv = gavg[:].rearrange("p (a b) -> p a b", b=GROUP)
            pl.affine_select(out=gv, in_=gv, compare_op=ALU.is_ge, fill=0.0, base=0,
                             pattern=[[-GROUP, P // GROUP], [0, GROUP]], channel_multiplier=1).then_inc(consts, 1)
            pl.wait_ge(consts, 5)
            pl.affine_select(out=gv, in_=gv, compare_op=ALU.is_ge, fill=0.0, base=GROUP - 1,
                             pattern=[[GROUP, P // GROUP], [0, GROUP]], channel_multiplier=-1).then_inc(consts, 1)
            pl.memset(xt[:], 0.0).then_inc(consts, 1)
            pl.memset(xn[:], 0.0).then_inc(consts, 1)

            for b in range(B):
                pl.wait_ge(tabled, (b + 1) * (16 * TT))
                with pl.Fori(0, PAIRS) as i:
                    for par2 in range(2):
                        c = 2 * i + (b * CHUNKS + par2)
                        pl.wait_ge(idx_ready, c + 1)
                        for k in range(TAPS):
                            pl.wait_ge(lerped, c * (TAPS * LERPS) + (k + 1) * LERPS)
                            alone(pl)
                            for t in range(TILES):
                                pl.indirect_dma_start(
                                    out=g[:, k, t].rearrange("p q c -> p (q c)"), out_offset=None, in_=tables[b],
                                    in_offset=bass.IndirectOffsetOnAxis(ap=idx[:, par2, t, k:k + 1], axis=0),
                                ).then_inc(gathered[k], 16)

        @block.tensor
        def _(pe):
            def group_stats(n):
                pe.wait_ge(mvr, 2 * n + 1)
                nc.tensor.matmul(ST[:, 0:1], gavg[:], mv[:, 0:1], start=True, stop=True).then_inc(gm_done, 1)
                pe.wait_ge(mvr, 2 * n + 2)
                nc.tensor.matmul(ST[:, 1:2], gavg[:], dev[:, 1:2], start=True, stop=True).then_inc(gm_done, 1)

            def turn_image(b):
                pe.wait_ge(xt_ready, b + 1)
                for j in range(TT // TG):
                    if j >= 2:
                        pe.wait_ge(tok_ready, b * (TT // TG) + (j - 1))
                    for t in range(TG):
                        n = (j * TG + t) * P
                        last = nc.tensor.transpose(PT[j % 2][:, t * P:(t + 1) * P], xt[:, n:n + P], ident[:])
                    last.then_inc(tok_turned, 1)

            def offset_conv(row):
                for k in range(TAPS):
                    last = nc.tensor.matmul(OM[0:27, 0:CP], woff[:, k, :],
                                            xn[:, bass.ds(row + k // 3, ROWS), k % 3:k % 3 + W],
                                            start=(k == 0), stop=(k == TAPS - 1))
                last.then_inc(om_ready, 1)

            def turn_offsets(n):
                pe.wait_ge(om_copied, n + 1)
                alone(pe)
                for t in range(TILES):
                    last = nc.tensor.transpose(OT[:, 32 * t:32 * t + 27], om[:, t * P:(t + 1) * P], ident[0:27, 0:27])
                last.then_inc(om_turned, 1)

            def conv_tap(c, k, par2):
                pe.wait_ge(copied, c * TAPS + (TAPS + k + 1))
                nc.tensor.matmul(CO[par2][:, 0:CP], wconv[:, k, :], cols[:, k % 2, :],
                                 start=(k == 0), stop=(k == TAPS - 1)).then_inc(conved, 1)

            def chunk(c, par2, row, ahead):
                if ahead:
                    offset_conv(row)
                pe.wait_ge(out_copied, c + 1)
                for k in range(TAPS):
                    pe.wait_ge(lerped, c * (TAPS * LERPS) + (TAPS * LERPS + (k + 1) * LERPS))
                    pe.wait_ge(copied, c * TAPS + (TAPS + k - 1))
                    for t in range(TILES):
                        last = nc.tensor.transpose(TP[k % 2][:, t * P:(t + 1) * P], acc[:, k % 3, t, :], ident[:])
                    last.then_inc(turned, 1)
                    if ahead and k == 2:
                        turn_offsets(c + 1)
                    if k:
                        conv_tap(c, k - 1, par2)
                conv_tap(c, TAPS - 1, par2)

            pe.wait_ge(consts, 8)
            group_stats(0)
            turn_image(0)
            pe.wait_ge(wo_in, 32)
            pe.wait_ge(xn_ready, 1)
            offset_conv(0)
            turn_offsets(0)
            pe.wait_ge(wc_in, 32)
            pe.wait_ge(granted, 1)

            with pe.Fori(0, B - 1) as b:
                group_stats(b + 1)
                turn_image(b + 1)
                pe.wait_ge(xn_ready, b + 2)
                alone(pe)
                with pe.Fori(0, PAIRS - 1) as i:
                    c = b * CHUNKS + 2 * i
                    chunk(c, 0, b * PW + i * (2 * ROWS) + ROWS, True)
                    chunk(c + 1, 1, b * PW + i * (2 * ROWS) + 2 * ROWS, True)
                c = b * CHUNKS + (CHUNKS - 2)
                chunk(c, 0, b * PW + (CHUNKS - 1) * ROWS, True)
                chunk(c + 1, 1, (b + 1) * PW, True)
            with pe.Fori(0, PAIRS - 1) as i:
                c = 2 * i + (B - 1) * CHUNKS
                chunk(c, 0, i * (2 * ROWS) + ((B - 1) * PW + ROWS), True)
                chunk(c + 1, 1, i * (2 * ROWS) + ((B - 1) * PW + 2 * ROWS), True)
            chunk(ALL - 2, 0, (B - 1) * PW + (CHUNKS - 1) * ROWS, True)
            chunk(ALL - 1, 1, None, False)

            def layer1_chunk(c, par2, row, normed_chunks):
                pe.wait_ge(normed, normed_chunks)
                pe.wait_ge(fin, c + 1)
                for k in range(TAPS):
                    last = nc.tensor.matmul(CO[par2][:, 0:CP], w1[:, k, :],
                                            xn[:, bass.ds(row + k // 3, ROWS), k % 3:k % 3 + W],
                                            start=(k == 0), stop=(k == TAPS - 1))
                last.then_inc(conv1, 1)

            def layer1(b, ahead):
                c = b * CHUNKS
                layer1_chunk(c, 0, b * PW, c + 2)
                layer1_chunk(c + 1, 1, b * PW + ROWS, c + 3)
                if ahead:
                    group_stats(b + (B + 1))
                with pe.Fori(1, PAIRS - 1) as i:
                    c = b * CHUNKS + 2 * i
                    layer1_chunk(c, 0, b * PW + i * (2 * ROWS), c + 2)
                    layer1_chunk(c + 1, 1, b * PW + i * (2 * ROWS) + ROWS, c + 3)
                layer1_chunk(b * CHUNKS + CHUNKS - 2, 0, b * PW + (CHUNKS - 2) * ROWS, b * CHUNKS + CHUNKS)
                layer1_chunk(b * CHUNKS + CHUNKS - 1, 1, b * PW + (CHUNKS - 1) * ROWS, b * CHUNKS + CHUNKS)

            pe.wait_ge(w1_in, 16)
            group_stats(B)
            with pe.Fori(0, B - 1) as b:
                layer1(b, True)
            layer1(B - 1, False)

        @block.scalar
        def _(act):
            def norm_xt(b):
                act.wait_ge(gn_ready, b + 1)
                nc.scalar.activation(xt[:].rearrange("p (r w) -> p r w", w=PW)[:, 1:1 + H, 1:1 + W],
                                     rows_of(x, b * HW, HW), ACT.Identity, scale=gn[:, 0:1], bias=gn[:, 1:2]).then_inc(xt_ready, 1)

            def copy_tok(b):
                act.wait_ge(tabled, b * (16 * TT))
                copy_tok_banks(b)

            def copy_tok_banks(b):
                for j in range(TT // TG):
                    act.wait_ge(tok_turned, b * (TT // TG) + (j + 1))
                    nc.scalar.activation(tok[:, j * TG:(j + 1) * TG, :].rearrange("p t c -> p (t c)"), PT[j % 2][:], ACT.Copy).then_inc(tok_ready, 1)

            def copy_offsets(n):
                act.wait_ge(om_ready, n + 1)
                nc.scalar.activation(om[:], OM[0:27, 0:CP], ACT.Identity, bias=boff[:]).then_inc(om_copied, 1)

            def masks(n):
                act.wait_ge(om_turned, n + 1)
                nc.scalar.activation(mask[:], OT[:, 0:96].rearrange("p (t n) -> p t n", n=32)[:, :, 18:27], ACT.Sigmoid).then_inc(mask_ready, 1)

            def copy_cols(c, k):
                act.wait_ge(turned, c * TAPS + (TAPS + k + 1))
                act.wait_ge(conved, c * TAPS + (TAPS + k - 1))
                nc.scalar.activation(cols[:, k % 2, :], TP[k % 2][:, 0:CP], ACT.Copy).then_inc(copied, 1)

            def chunk(c, par2, ahead):
                act.wait_ge(idx_ready, c + 1)
                for k in range(TAPS):
                    act.wait_ge(gathered[k], c * (16 * TILES) + 16 * TILES)
                    act.wait_ge(turned, c * TAPS + (TAPS + k - 2))
                    for t in range(TILES):
                        nc.scalar.activation(acc[:, k % 3, t, :], g[:, k, t, 0, :], ACT.Copy,
                                             scale=wt[:, par2, 0, t, k:k + 1]).then_inc(scaled, 1)
                    if k:
                        copy_cols(c, k - 1)
                    if ahead and k == 1:
                        copy_offsets(c + 1)
                    if ahead and k == 3:
                        masks(c + 1)
                copy_cols(c, TAPS - 1)
                act.wait_ge(conved, c * TAPS + 2 * TAPS)
                nc.scalar.activation(o[:, bass.ds(c * CP, CP)], CO[par2][:, 0:CP], ACT.Identity, bias=par[:, 0:1]).then_inc(out_copied, 1)

            act.wait_ge(consts, 8)
            act.wait_ge(x0_in, 16)
            norm_xt(0)
            copy_tok_banks(0)
            act.wait_ge(wo_in, 32)
            copy_offsets(0)
            masks(0)
            act.wait_ge(granted, 1)
            act.wait_ge(wc_in, 32)
            act.wait_ge(xr_in, 16)
            with act.Fori(0, B - 1) as b:
                norm_xt(b + 1)
                copy_tok(b + 1)
                with act.Fori(0, PAIRS) as i:
                    chunk(b * CHUNKS + 2 * i, 0, True)
                    chunk(b * CHUNKS + 2 * i + 1, 1, True)
            with act.Fori(0, PAIRS - 1) as i:
                chunk(2 * i + (B - 1) * CHUNKS, 0, True)
                chunk(2 * i + ((B - 1) * CHUNKS + 1), 1, True)
            chunk(ALL - 2, 0, True)
            chunk(ALL - 1, 1, False)

            act.wait_ge(bn_ready, 1)
            with act.Fori(0, B) as b:
                with act.Fori(0, CHUNKS) as j:
                    s = b * HW + j * CP
                    nc.scalar.activation(o[:, bass.ds(s, CP)], o[:, bass.ds(s, CP)], ACT.Relu, scale=bna[:, 0:1], bias=bna[:, 1:2]).then_inc(relued, 1)
                act.wait_ge(gn_ready, b + (B + 1))
                with act.Fori(0, CHUNKS) as j:
                    nc.scalar.activation(interior(xn, b * PW + j * ROWS + 1, ROWS), rows_of(x, b * HW + j * CP, CP), ACT.Identity,
                                         scale=gn[:, 0:1], bias=gn[:, 1:2]).then_inc(normed, 1)

        @block.vector
        def _(dve):
            def rsqrt(n, out, var):
                done = [0]

                def step(ins):
                    done[0] += 1
                    ins.then_inc(rs, 1)
                    dve.wait_ge(rs, n * RSTEPS + done[0])

                v, y, t = rq[:, 0:1], rq[:, 1:2], rq[:, 2:3]
                step(nc.vector.tensor_scalar(v, var, EPS, None, ALU.add))
                step(nc.vector.tensor_scalar(t.bitcast(I32), v.bitcast(I32), 1, None, ALU.arith_shift_right))
                step(nc.vector.tensor_scalar(y.bitcast(I32), t.bitcast(I32), -1.0, float(0x5F3759DF), ALU.mult, ALU.add))
                for i in range(NEWTON):
                    step(nc.vector.tensor_tensor(t, y, y, ALU.mult))
                    step(nc.vector.scalar_tensor_tensor(t, t, -0.5, v, ALU.mult, ALU.mult))
                    step(nc.vector.scalar_tensor_tensor(out if i == NEWTON - 1 else y, t, 1.5, y, ALU.add, ALU.mult))

            def group_norm(n, s0, nr):
                nc.vector.bn_aggr(mv[:], bst[:].rearrange("p a b -> p (a b)")).then_inc(mvr, 1)
                dve.wait_ge(gm_done, 2 * n + 1)
                dve.wait_ge(mvr, 2 * n + 1)
                nc.vector.tensor_tensor(dev[:, 0:1], mv[:, 0:1], ST[:, 0:1], ALU.subtract).then_inc(st, 1)
                dve.wait_ge(st, s0 + 1)
                nc.vector.scalar_tensor_tensor(dev[:, 1:2], dev[:, 0:1], dev[:, 0:1], mv[:, 1:2], ALU.mult, ALU.add).then_inc(mvr, 1)
                dve.wait_ge(gm_done, 2 * n + 2)
                rsqrt(nr, gn[:, 0:1], ST[:, 1:2])
                nc.vector.scalar_tensor_tensor(gn[:, 1:2], ST[:, 0:1], -1.0, gn[:, 0:1], ALU.mult, ALU.mult).then_inc(gn_ready, 1)

            def prepare(b):
                s0 = b * (CHUNKS + 1)
                for j in range(CHUNKS):
                    nc.vector.bn_stats(bst[:, j, :], x[:, bass.ds(b * HW + j * CP, CP)]).then_inc(st, 1)
                dve.wait_ge(st, s0 + CHUNKS)
                alone(dve)
                group_norm(b, s0 + CHUNKS, b)
                dve.wait_ge(gn_ready, b + 1)
                nc.vector.tensor_scalar(interior(xn, b * PW + 1, H), rows_of(x, b * HW, HW), gn[:, 0:1], gn[:, 1:2],
                                        ALU.mult, ALU.add).then_inc(xn_ready, 1)

            STEPS = 14

            def indices(n, b, j, par2):
                done = [0]

                def step(ins):
                    done[0] += 1
                    ins.then_inc(ix, 1)
                    dve.wait_ge(ix, n * STEPS + done[0])

                dve.wait_ge(mask_ready, n + 1)
                ot = OT[:, 0:96].rearrange("p (t n) -> p t n", n=32)
                step(nc.vector.tensor_tensor(pos[:], ot[:, :, 0:18], grid[:, j] if isinstance(j, int) else grid[:, bass.ds(j, 1)].rearrange("p a t n -> p (a t) n"), ALU.add))
                step(nc.vector.tensor_scalar(pos[:], pos[:], -1.0, float(H), ALU.max, ALU.min))
                step(nc.vector.tensor_scalar(low[:], pos[:], -0.5, ROUND, ALU.add, ALU.add))
                step(nc.vector.tensor_scalar(low[:], low[:], -ROUND, -1.0, ALU.add, ALU.max))
                step(nc.vector.tensor_scalar(low[:], low[:], float(H - 1), None, ALU.min))
                step(nc.vector.tensor_tensor(frac[:], pos[:], low[:], ALU.subtract))
                step(nc.vector.tensor_scalar(rest[:], frac[:], -1.0, 1.0, ALU.mult, ALU.add))
                step(nc.vector.scalar_tensor_tensor(idxf[:], low[:, :, 0:9], float(PW), low[:, :, 9:18], ALU.mult, ALU.add))
                nc.vector.tensor_scalar(idx[:, par2], idxf[:], float(LEAD + PW + 1), None, ALU.add).then_inc(ix, 1)
                done[0] += 1
                nc.vector.tensor_tensor(my[:, 0], mask[:], rest[:, :, 0:9], ALU.mult).then_inc(ix, 1)
                done[0] += 1
                step(nc.vector.tensor_tensor(my[:, 1], mask[:], frac[:, :, 0:9], ALU.mult))
                for q in range(4):
                    last = nc.vector.tensor_tensor(wt[:, par2, q], my[:, q // 2], (frac if q % 2 else rest)[:, :, 9:18], ALU.mult)
                    if q < 3:
                        last.then_inc(ix, 1)
                        done[0] += 1
                last.then_inc(idx_ready, 1)
                assert done[0] == STEPS

            def chunk(c, par2, nb, nj, ahead):
                dve.wait_ge(idx_ready, c + 1)
                for k in range(TAPS):
                    dve.wait_ge(gathered[k], c * (16 * TILES) + 16 * TILES)
                    for q in range(1, 4):
                        for t in range(TILES):
                            if q == 1:
                                dve.wait_ge(scaled, c * (TAPS * TILES) + (TAPS * TILES + k * TILES + t + 1))
                            else:
                                dve.wait_ge(lerped, c * (TAPS * LERPS) + (TAPS * LERPS + k * LERPS + (q - 2) * TILES + t + 1))
                            a = acc[:, k % 3, t, :]
                            nc.vector.scalar_tensor_tensor(a, g[:, k, t, q, :], wt[:, par2, q, t, k:k + 1], a,
                                                           ALU.mult, ALU.add).then_inc(lerped, 1)
                    if ahead and k == 4:
                        indices(c + 1, nb, nj, 1 - par2)
                dve.wait_ge(out_copied, c + 3)
                nc.vector.bn_stats(ost[:, bass.ds(c, 1), :].rearrange("p a n -> p (a n)"), o[:, bass.ds(c * CP, CP)]).then_inc(ostat, 1)

            dve.wait_ge(x0_in, 16)
            dve.wait_ge(consts, 8)
            prepare(0)
            dve.wait_ge(gr_in, 16)
            indices(0, 0, 0, 0)
            dve.wait_ge(granted, 1)
            dve.wait_ge(xr_in, 16)
            with dve.Fori(0, B - 1) as b:
                prepare(b + 1)
                with dve.Fori(0, PAIRS - 1) as i:
                    chunk(b * CHUNKS + 2 * i, 0, b, 2 * i + 1, True)
                    chunk(b * CHUNKS + 2 * i + 1, 1, b, 2 * i + 2, True)
                chunk(b * CHUNKS + (CHUNKS - 2), 0, b, CHUNKS - 1, True)
                chunk(b * CHUNKS + (CHUNKS - 1), 1, b + 1, 0, True)
            with dve.Fori(0, PAIRS - 1) as i:
                chunk(2 * i + (B - 1) * CHUNKS, 0, B - 1, 2 * i + 1, True)
                chunk(2 * i + ((B - 1) * CHUNKS + 1), 1, B - 1, 2 * i + 2, True)
            chunk(ALL - 2, 0, B - 1, CHUNKS - 1, True)
            chunk(ALL - 1, 1, None, None, False)

            dve.wait_ge(ostat, ALL)
            dve.wait_ge(wc_in, 32)
            nc.vector.bn_aggr(omv[:], ost[:].rearrange("p a b -> p (a b)")).then_inc(ostat, 1)
            dve.wait_ge(ostat, ALL + 1)
            rsqrt(B, bna[:, 2:3], omv[:, 1:2])
            dve.wait_ge(rs, (B + 1) * RSTEPS)
            nc.vector.tensor_tensor(bna[:, 0:1], bna[:, 2:3], par[:, 1:2], ALU.mult).then_inc(ostat, 1)
            dve.wait_ge(ostat, ALL + 2)
            nc.vector.tensor_tensor(bna[:, 2:3], omv[:, 0:1], bna[:, 0:1], ALU.mult).then_inc(ostat, 1)
            dve.wait_ge(ostat, ALL + 3)
            nc.vector.tensor_tensor(bna[:, 1:2], par[:, 2:3], bna[:, 2:3], ALU.subtract).then_inc(bn_ready, 1)

            ST0 = B * (CHUNKS + 1)

            def residual(b):
                s0 = b * (CHUNKS + 1) + ST0
                with dve.Fori(0, CHUNKS) as j:
                    n = b * CHUNKS + j
                    dve.wait_ge(relued, n + 1)
                    xs = x[:, bass.ds(n * CP, CP)]
                    nc.vector.tensor_tensor(xs, xs, o[:, bass.ds(n * CP, CP)], ALU.add).then_inc(summed, 1)
                    dve.wait_ge(summed, n + 1)
                    nc.vector.bn_stats(bst[:, bass.ds(j, 1), :].rearrange("p a n -> p (a n)"), xs).then_inc(st, 1)
                dve.wait_ge(st, s0 + CHUNKS)
                alone(dve)
                group_norm(b + B, s0 + CHUNKS, b + (B + 1))

            def finish(b):
                with dve.Fori(0, PAIRS) as i:
                    for par2 in range(2):
                        c = b * CHUNKS + 2 * i + par2
                        dve.wait_ge(conv1, c + 1)
                        xs = x[:, bass.ds(c * CP, CP)]
                        nc.vector.scalar_tensor_tensor(xs, CO[par2][:, 0:CP], par[:, 3:4], xs, ALU.add, ALU.add).then_inc(fin, 1)

            residual(0)
            with dve.Fori(0, B - 1) as b:
                dve.wait_ge(normed, (b + 1) * CHUNKS)
                alone(dve)
                residual(b + 1)
                finish(b)
            finish(B - 1)


_LAYOUT = "weights with input channels first; offsets as 9 dy, 9 dx, 9 mask rows"


def kernel(x, L0_conv_w_offset, L0_conv_b_offset, L0_conv_w_conv, L0_conv_b_conv, L0_conv_gamma, L0_conv_beta,
           L1_conv_weight, L1_conv_bias):
    import numpy as np
    import concourse.bacc as bacc
    from concourse.bass_utils import run_bass_kernel_spmd as run

    def taps_first(w):
        return np.ascontiguousarray(np.transpose(w, (1, 2, 3, 0))).reshape(P, TAPS, w.shape[0])

    order = [2 * k for k in range(9)] + [2 * k + 1 for k in range(9)] + list(range(18, 27))
    n = np.arange(HW).reshape(CHUNKS * TILES, P).T
    k = np.arange(TAPS)
    gy = (n // W)[:, :, None] + (k // 3 - 1)[None, None, :]
    gx = (n % W)[:, :, None] + (k % 3 - 1)[None, None, :]
    grid = np.concatenate([gy, gx], axis=2).astype(np.float32).reshape(P, CHUNKS, TILES, 18)
    arrays = {
        "x_dram": np.ascontiguousarray(np.transpose(np.asarray(x), (1, 0, 2, 3))).reshape(P, B, HW),
        "woff_dram": taps_first(np.asarray(L0_conv_w_offset)[order]),
        "wconv_dram": taps_first(np.asarray(L0_conv_w_conv)),
        "w1_dram": taps_first(np.asarray(L1_conv_weight)),
        "boff_dram": np.ascontiguousarray(np.asarray(L0_conv_b_offset)[order]).reshape(27, 1),
        "par_dram": np.ascontiguousarray(np.stack([np.asarray(v) for v in (
            L0_conv_b_conv, L0_conv_gamma, L0_conv_beta, L1_conv_bias, L1_conv_bias)], axis=1)),
        "grid_dram": grid,
    }
    nc = bacc.Bacc("TRN2", target_bir_lowering=False, num_devices=1)
    aps = [nc.dram_tensor(name, a.shape, F32, kind="ExternalInput").ap() for name, a in arrays.items()]
    out = nc.dram_tensor("out_dram", (P, B * HW), F32, kind="ExternalOutput").ap()
    build(nc, *aps, out)
    r = run(nc, [arrays], core_ids=[0])
    y = r.results[0]["out_dram"].reshape(P, B, H, W)
    return np.ascontiguousarray(np.transpose(y, (1, 0, 2, 3)))
```

```python
import concourse.bass as bass
from concourse import mybir
from contextlib import ExitStack

F32 = mybir.dt.float32
I32 = mybir.dt.int32
ALU = mybir.AluOpType
ACT = mybir.ActivationFunctionType

P = 128
B, H, W = 4, 48, 48
HW = H * W
TAPS = 9
PW = W + 2
TILES = 3
CP = TILES * P
ROWS = CP // W
CHUNKS = HW // CP
PAIRS = CHUNKS // 2
ALL = B * CHUNKS
GROUP = 4
EPS = 1e-5
TT = 20
TG = 4
LEAD = 64
TABLE = LEAD + TT * P
ROUND = 12582912.0
NEWTON = 3
RSTEPS = 3 + 3 * NEWTON
LERPS = 3 * TILES
BANDS = 4
BR = H // BANDS
BP = BR * W
HB = BP // 2
HALF = W // 2
MIX = 4


def build(nc, x_d, woff_d, wconv_d, w1_d, boff_d, par_d, grid_d, out_d):
    tables = [nc.dram_tensor(f"corner_table{b}", [TABLE, 4 * P], F32, kind="Internal").ap() for b in range(B)]

    with ExitStack() as ctx:
        def sb(name, shape, dt=F32):
            return ctx.enter_context(nc.sbuf_tensor(name, shape, dt))

        def ps(name):
            return ctx.enter_context(nc.psum_tensor(name, [P, 512], F32))

        def sem(name):
            return ctx.enter_context(nc.semaphore(name))

        x = sb("x", [P, B * HW])
        o = sb("o", [P, B * HW])
        xn = sb("xn", [P, B * PW, PW])
        xt = sb("xt", [P, 52 * PW])
        tok = sb("tok", [P, TT, P])
        g = sb("g", [P, TAPS, TILES, 4, P])
        mixed = g[:].rearrange("p k t q c -> p (k t q c)")[:, 0:MIX * PW * HALF].rearrange("p (m r w) -> p m r w", m=MIX, w=HALF)
        acc = sb("acc", [P, 3, TILES, P])
        cols = sb("cols", [P, 2, CP])
        woff = sb("woff", [P, TAPS, 27])
        wconv = sb("wconv", [P, TAPS, P])
        w1 = tok[:, 0:TAPS, :]
        w1_rows = w1.rearrange("p (y x) c -> p y x c", x=3)
        w_plus, w_minus, w_outer = tok[:, 9:12, :], tok[:, 12:15, :], tok[:, 15:18, :]
        boff = sb("boff", [27, 1])
        par = sb("par", [P, 5])
        grid = sb("grid", [P, CHUNKS, TILES, 18])
        ident = sb("ident", [P, P])
        gavg = sb("gavg", [P, P])
        om = sb("om", [27, CP])
        mask = sb("mask", [P, TILES, 9])
        pos = sb("pos", [P, TILES, 18])
        low = sb("low", [P, TILES, 18])
        frac = sb("frac", [P, TILES, 18])
        rest = sb("rest", [P, TILES, 18])
        my = sb("my", [P, 2, TILES, 9])
        idxf = sb("idxf", [P, TILES, 9])
        idx = sb("idx", [P, 2, TILES, 9], I32)
        wt = sb("wt", [P, 2, 4, TILES, 9])
        bst = sb("bst", [P, 2 * BANDS, 6])
        mv = sb("mv", [P, 2])
        dev = sb("dev", [P, 2])
        gn = sb("gn", [P, 2 * B, 2])
        ost = sb("ost", [P, ALL, 6])
        omv = sb("omv", [P, 2])
        rq = sb("rq", [P, 3])
        bna = sb("bna", [P, 4])

        OM, OT, TP0, TP1, CO0, CO1, PT0, PT1 = (ps(n) for n in ("OM", "OT", "TP0", "TP1", "CO0", "CO1", "PT0", "PT1"))
        TP, CO, PT = (TP0, TP1), (CO0, CO1), (PT0, PT1)
        ST0, ST1 = OT[:, 500:502], OM[:, 500:502]
        MX = ((OM, OT, TP0, TP1), (CO0, CO1, PT0, PT1))

        x0a_in, x0b_in, xr_in, wo_in, wc_in, w1_in, gr_in = (sem(n) for n in ("x0a_in", "x0b_in", "xr_in", "wo_in", "wc_in", "w1_in", "gr_in"))
        consts = sem("consts")
        st = sem("st")
        dv = sem("dv")
        gm_done = sem("gm_done")
        gn_ready = sem("gn_ready")
        mvr = sem("mvr")
        xt_ready = sem("xt_ready")
        xn_ready = sem("xn_ready")
        tok_turned = sem("tok_turned")
        tok_ready = sem("tok_ready")
        ends = sem("ends")
        tabled = sem("tabled")
        om_ready = sem("om_ready")
        om_copied = sem("om_copied")
        om_turned = sem("om_turned")
        mask_ready = sem("mask_ready")
        idx_ready = sem("idx_ready")
        gathered = [sem(f"gathered{k}") for k in range(TAPS)]
        scaled = sem("scaled")
        lerped = sem("lerped")
        turned = sem("turned")
        copied = sem("copied")
        conved = sem("conved")
        out_copied = sem("out_copied")
        granted = sem("granted")
        passed = sem("passed")
        ix = sem("ix")
        rs = sem("rs")
        ostat = sem("ostat")
        warm = sem("warm")
        bn_ready = sem("bn_ready")
        w_mixed = sem("w_mixed")
        relued = sem("relued")
        added = sem("added")
        normed = sem("normed")
        mixed0 = sem("mixed0")
        mixed_ready = sem("mixed_ready")
        conv1 = sem("conv1")
        unmixed = sem("unmixed")
        fin = sem("fin")
        stored = sem("stored")

        block = ctx.enter_context(nc.Block())

        def interior(t, row, rows):
            return t[:, bass.ds(row, rows), 1:1 + W]

        def gn_of(n, i):
            return gn[:, bass.ds(n, 1), i]

        def rows_of(t, start, n):
            return t[:, bass.ds(start, n)].rearrange("p (r w) -> p r w", w=W)

        def mix(eng, b, h, m):
            first, rows = (0, BR + 2) if h == 0 else (h * BR + 2, BR)
            src = xn[:, bass.ds(b * PW + first, rows), :]
            d0, d2 = src[:, :, 0:W:2], src[:, :, 2:PW:2]
            d1, d3 = src[:, :, 1:W:2], src[:, :, 3:PW:2]
            p, q, op = ((d0, d2, ALU.subtract), (d1, d2, ALU.add), (d2, d1, ALU.subtract), (d1, d3, ALU.subtract))[m]
            return eng.tensor_tensor(mixed[:, m, first:first + rows, :], p, q, op)

        def alone(eng):
            eng.sem_inc(passed, 1)

        @block.sync
        def _(sp):
            sp.sem_inc(scaled, TAPS * TILES)
            sp.sem_inc(lerped, TAPS * LERPS)
            sp.sem_inc(turned, TAPS)
            sp.sem_inc(copied, TAPS)
            sp.sem_inc(conved, TAPS)
            sp.sem_inc(out_copied, 2)
            sp.sem_inc(fin, 4)
            sp.sem_inc(conv1, MIX * BANDS)
            sp.sem_inc(granted, 1)
            sp.dma_start(x[:, 0:HW // 2], x_d[:, 0, 0:HW // 2]).then_inc(x0a_in, 16)
            sp.dma_start(x[:, HW // 2:HW], x_d[:, 0, HW // 2:]).then_inc(x0b_in, 16)
            sp.dma_start(woff[:], woff_d).then_inc(wo_in, 16)
            sp.dma_start(boff[:], boff_d).then_inc(wo_in, 16)
            sp.dma_start(grid[:], grid_d).then_inc(gr_in, 16)
            sp.dma_start(x[:, HW:].rearrange("p (b n) -> p b n", b=B - 1), x_d[:, 1:B]).then_inc(xr_in, 16)
            sp.dma_start(wconv[:], wconv_d).then_inc(wc_in, 16)
            sp.dma_start(par[:], par_d).then_inc(wc_in, 16)
            sp.wait_ge(consts, 11)
            zeros = acc[0:LEAD].rearrange("p a t c -> p (a t c)")[:, 0:4 * P]
            for b in range(B):
                sp.dma_start(tables[b][0:LEAD], zeros).then_inc(ends, 16)
                sp.dma_start(tables[b][TABLE - LEAD:TABLE], zeros).then_inc(ends, 16)
            sp.wait_ge(ends, 2 * B * 16)
            for b in range(B):
                for j in range(TT // TG):
                    sp.wait_ge(tok_ready, b * (TT // TG) + (j + 1))
                    for q in range(4):
                        shift = PW * (q // 2) + q % 2
                        row = LEAD + j * TG * P - shift
                        dst = tables[b][row:row + TG * P, q * P:(q + 1) * P]
                        sp.dma_start(dst.rearrange("(t p) c -> p t c", p=P), tok[:, j * TG:(j + 1) * TG, :]).then_inc(tabled, 16)
            sp.wait_ge(tabled, B * 16 * TT)
            sp.dma_start(w1, w1_d).then_inc(w1_in, 16)
            with sp.Fori(0, B * BANDS) as i:
                sp.wait_ge(fin, 2 * i + 6)
                sp.dma_start(out_d[:, bass.ds(i * BP, BP)], x[:, bass.ds(i * BP, BP)]).then_inc(stored, 16)
            sp.wait_ge(stored, 16 * B * BANDS)

        @block.gpsimd
        def _(pl):
            xn4 = xn[:].rearrange("p (b r) w -> p b r w", b=B)
            xt3 = xt[:].rearrange("p (r w) -> p r w", w=PW)
            pl.memset(xt3[:, 0:1], 0.0).then_inc(consts, 1)
            pl.memset(xt3[:, 1 + H:], 0.0).then_inc(consts, 1)
            pl.memset(xt3[:, 1:1 + H, 0:PW:PW - 1], 0.0).then_inc(consts, 1)
            pl.memset(xn4[:, :, 0:PW:PW - 1, :], 0.0).then_inc(consts, 1)
            pl.memset(xn4[:, :, 1:1 + H, 0:PW:PW - 1], 0.0).then_inc(consts, 1)
            pl.memset(acc[:], 0.0).then_inc(consts, 1)
            pl.memset(ident[:], 0.0).then_inc(consts, 1)
            pl.memset(gavg[:], 1.0 / GROUP).then_inc(consts, 1)
            pl.wait_ge(consts, 8)
            pl.affine_select(out=ident[:], in_=ident[:], compare_op=ALU.not_equal, fill=1.0, base=0,
                             pattern=[[-1, P]], channel_multiplier=1).then_inc(consts, 1)
            gv = gavg[:].rearrange("p (a b) -> p a b", b=GROUP)
            pl.affine_select(out=gv, in_=gv, compare_op=ALU.is_ge, fill=0.0, base=0,
                             pattern=[[-GROUP, P // GROUP], [0, GROUP]], channel_multiplier=1).then_inc(consts, 1)
            pl.wait_ge(consts, 10)
            pl.affine_select(out=gv, in_=gv, compare_op=ALU.is_ge, fill=0.0, base=GROUP - 1,
                             pattern=[[GROUP, P // GROUP], [0, GROUP]], channel_multiplier=-1).then_inc(consts, 1)

            for b in range(B):
                pl.wait_ge(tabled, (b + 1) * (16 * TT))
                with pl.Fori(0, PAIRS) as i:
                    for par2 in range(2):
                        c = 2 * i + (b * CHUNKS + par2)
                        pl.wait_ge(idx_ready, c + 1)
                        for k in range(TAPS):
                            pl.wait_ge(lerped, c * (TAPS * LERPS) + (k + 1) * LERPS)
                            alone(pl)
                            for t in range(TILES):
                                pl.indirect_dma_start(
                                    out=g[:, k, t].rearrange("p q c -> p (q c)"), out_offset=None, in_=tables[b],
                                    in_offset=bass.IndirectOffsetOnAxis(ap=idx[:, par2, t, k:k + 1], axis=0),
                                ).then_inc(gathered[k], 16)

            def add(b):
                for j in range(BANDS):
                    pl.wait_ge(relued, b * BANDS + (j + 1))
                    xs = x[:, bass.ds(b * HW + j * BP, BP)]
                    pl.tensor_tensor(xs, xs, o[:, bass.ds(b * HW + j * BP, BP)], ALU.add).then_inc(added, 1)

            def mix_band(b, h):
                pl.wait_ge(normed, b * BANDS + (h + 1))
                pl.wait_ge(conv1, MIX * (b * BANDS + min(h + 2, BANDS)))
                for m in range(MIX):
                    mix(pl, b, h, m).then_inc(mixed_ready, 1)

            add(0)
            with pl.Fori(0, B - 1) as b:
                for h in range(1, BANDS):
                    mix_band(b, h)
                add(b + 1)
                mix_band(b + 1, 0)
            for h in range(1, BANDS):
                mix_band(B - 1, h)

        @block.tensor
        def _(pe):
            def group_mean(n, ST):
                pe.wait_ge(mvr, 2 * n + 1)
                nc.tensor.matmul(ST[:, 0:1], gavg[:], mv[:, 0:1], start=True, stop=True).then_inc(gm_done, 1)

            def group_var(n, ST):
                pe.wait_ge(mvr, 2 * n + 2)
                nc.tensor.matmul(ST[:, 1:2], gavg[:], dev[:, 1:2], start=True, stop=True).then_inc(gm_done, 1)

            def group_stats(n):
                group_mean(n, ST0)
                group_var(n, ST0)

            def turn_image(b):
                pe.wait_ge(xt_ready, b + 1)
                for j in range(TT // TG):
                    if j >= 2:
                        pe.wait_ge(tok_ready, b * (TT // TG) + (j - 1))
                    for t in range(TG):
                        n = (j * TG + t) * P
                        last = nc.tensor.transpose(PT[j % 2][:, t * P:(t + 1) * P], xt[:, n:n + P], ident[:])
                    last.then_inc(tok_turned, 1)

            def offset_conv(row, taps=range(TAPS)):
                for k in taps:
                    last = nc.tensor.matmul(OM[0:27, 0:CP], woff[:, k, :],
                                            xn[:, bass.ds(row + k // 3, ROWS), k % 3:k % 3 + W],
                                            start=(k == 0), stop=(k == TAPS - 1))
                if taps[-1] == TAPS - 1:
                    last.then_inc(om_ready, 1)

            def turn_offsets(n):
                pe.wait_ge(om_copied, n + 1)
                alone(pe)
                for t in range(TILES):
                    last = nc.tensor.transpose(OT[:, 32 * t:32 * t + 27], om[:, t * P:(t + 1) * P], ident[0:27, 0:27])
                last.then_inc(om_turned, 1)

            def conv_tap(c, k, par2):
                pe.wait_ge(copied, c * TAPS + (TAPS + k + 1))
                nc.tensor.matmul(CO[par2][:, 0:CP], wconv[:, k, :], cols[:, (par2 + k) % 2, :],
                                 start=(k == 0), stop=(k == TAPS - 1)).then_inc(conved, 1)

            def chunk(c, par2, row, drain, ahead):
                for k in range(TAPS):
                    if ahead and k < 3:
                        offset_conv(row, range(3 * k, 3 * k + 3))
                    if drain and k == 0:
                        conv_tap(c - 1, TAPS - 1, 1 - par2)
                    pe.wait_ge(lerped, c * (TAPS * LERPS) + (TAPS * LERPS + (k + 1) * LERPS))
                    pe.wait_ge(copied, c * TAPS + (TAPS + k - 1))
                    for t in range(TILES):
                        last = nc.tensor.transpose(TP[(par2 + k) % 2][:, t * P:(t + 1) * P], acc[:, k % 3, t, :], ident[:])
                    last.then_inc(turned, 1)
                    if k == 1:
                        pe.wait_ge(out_copied, c + 1)
                    if k:
                        conv_tap(c, k - 1, par2)
                    if ahead and k == 3:
                        turn_offsets(c + 1)

            pe.wait_ge(consts, 11)
            group_stats(0)
            turn_image(0)
            pe.wait_ge(wo_in, 32)
            pe.wait_ge(xn_ready, 1)
            offset_conv(0)
            turn_offsets(0)
            with pe.Fori(1, B) as b:
                group_stats(b)
            pe.wait_ge(wc_in, 32)
            pe.wait_ge(granted, 1)

            chunk(0, 0, ROWS, False, True)
            with pe.Fori(0, B - 1) as b:
                turn_image(b + 1)
                pe.wait_ge(xn_ready, b + 2)
                alone(pe)
                with pe.Fori(0, PAIRS - 1) as i:
                    c = b * CHUNKS + 2 * i
                    chunk(c + 1, 1, b * PW + i * (2 * ROWS) + 2 * ROWS, True, True)
                    chunk(c + 2, 0, b * PW + i * (2 * ROWS) + 3 * ROWS, True, True)
                c = b * CHUNKS + (CHUNKS - 1)
                chunk(c, 1, (b + 1) * PW, True, True)
                chunk(c + 1, 0, (b + 1) * PW + ROWS, True, True)
            with pe.Fori(0, PAIRS - 1) as i:
                c = 2 * i + (B - 1) * CHUNKS
                chunk(c + 1, 1, i * (2 * ROWS) + ((B - 1) * PW + 2 * ROWS), True, True)
                chunk(c + 2, 0, i * (2 * ROWS) + ((B - 1) * PW + 3 * ROWS), True, True)
            chunk(ALL - 1, 1, None, True, False)
            conv_tap(ALL - 1, TAPS - 1, 1)

            def layer1_band(n, h, first, stats=None):
                pe.wait_ge(fin, 2 * n + 2)
                for m in range(MIX):
                    if first:
                        pe.wait_ge(mixed0, m + 1)
                    else:
                        pe.wait_ge(mixed_ready, MIX * n + (m + 1 - MIX))
                    for ky in range(3):
                        w = (w1_rows[:, ky, 0], w_plus[:, ky], w_minus[:, ky], w1_rows[:, ky, 2])[m]
                        r = h * BR + ky
                        last = nc.tensor.matmul(MX[h % 2][m][:, 0:HB], w, mixed[:, m, r:r + BR, :], start=(ky == 0), stop=(ky == 2))
                    last.then_inc(conv1, 1)
                    if stats is not None and m == 0:
                        group_mean(stats, ST1)
                    if stats is not None and m == 1:
                        group_var(stats, ST1)

            pe.wait_ge(w_mixed, 4)
            group_mean(B, ST1)
            group_var(B, ST1)
            layer1_band(0, 0, True)
            with pe.Fori(0, B - 1) as b:
                layer1_band(b * BANDS + 1, 1, False)
                layer1_band(b * BANDS + 2, 2, False, b + (B + 1))
                layer1_band(b * BANDS + 3, 3, False)
                layer1_band(b * BANDS + 4, 0, False)
            for h in range(1, BANDS):
                layer1_band((B - 1) * BANDS + h, h, False)

        @block.scalar
        def _(act):
            def norm_xn(b):
                act.wait_ge(gn_ready, b + 1)
                nc.scalar.activation(interior(xn, b * PW + 1, H), rows_of(x, b * HW, HW), ACT.Identity,
                                     scale=gn_of(b, 0), bias=gn_of(b, 1)).then_inc(xn_ready, 1)

            def copy_tok(b):
                act.wait_ge(tabled, b * (16 * TT))
                copy_tok_banks(b)

            def copy_tok_banks(b):
                for j in range(TT // TG):
                    act.wait_ge(tok_turned, b * (TT // TG) + (j + 1))
                    nc.scalar.activation(tok[:, j * TG:(j + 1) * TG, :].rearrange("p t c -> p (t c)"), PT[j % 2][:], ACT.Copy).then_inc(tok_ready, 1)

            def copy_offsets(n):
                act.wait_ge(om_ready, n + 1)
                nc.scalar.activation(om[:], OM[0:27, 0:CP], ACT.Identity, bias=boff[:]).then_inc(om_copied, 1)

            def masks(n):
                act.wait_ge(om_turned, n + 1)
                nc.scalar.activation(mask[:], OT[:, 0:96].rearrange("p (t n) -> p t n", n=32)[:, :, 18:27], ACT.Sigmoid).then_inc(mask_ready, 1)

            def copy_cols(c, k, par2):
                act.wait_ge(turned, c * TAPS + (TAPS + k + 1))
                act.wait_ge(conved, c * TAPS + (TAPS + k - 1))
                nc.scalar.activation(cols[:, (par2 + k) % 2, :], TP[(par2 + k) % 2][:, 0:CP], ACT.Copy).then_inc(copied, 1)

            def copy_out(c, par2):
                act.wait_ge(conved, c * TAPS + 2 * TAPS)
                nc.scalar.activation(o[:, bass.ds(c * CP, CP)], CO[par2][:, 0:CP], ACT.Identity, bias=par[:, 0:1]).then_inc(out_copied, 1)

            def chunk(c, par2, drain, ahead):
                act.wait_ge(idx_ready, c + 1)
                for k in range(TAPS):
                    act.wait_ge(gathered[k], c * (16 * TILES) + 16 * TILES)
                    act.wait_ge(turned, c * TAPS + (TAPS + k - 2))
                    for t in range(TILES):
                        nc.scalar.activation(acc[:, k % 3, t, :], g[:, k, t, 0, :], ACT.Copy,
                                             scale=wt[:, par2, 0, t, k:k + 1]).then_inc(scaled, 1)
                    if drain and k == 0:
                        copy_cols(c - 1, TAPS - 1, 1 - par2)
                    if drain and k == 1:
                        copy_out(c - 1, 1 - par2)
                    if k:
                        copy_cols(c, k - 1, par2)
                    if ahead and k == 3:
                        copy_offsets(c + 1)
                    if ahead and k == 4:
                        masks(c + 1)

            act.wait_ge(consts, 11)
            nc.scalar.activation(mask[:], acc[:, 0, :, 0:9], ACT.Sigmoid).then_inc(warm, 1)
            act.wait_ge(x0b_in, 16)
            norm_xn(0)
            copy_tok_banks(0)
            act.wait_ge(wo_in, 32)
            copy_offsets(0)
            masks(0)
            act.wait_ge(granted, 1)
            act.wait_ge(wc_in, 32)
            act.wait_ge(xr_in, 16)
            chunk(0, 0, False, True)
            with act.Fori(0, B - 1) as b:
                norm_xn(b + 1)
                copy_tok(b + 1)
                with act.Fori(0, PAIRS) as i:
                    chunk(b * CHUNKS + 2 * i + 1, 1, True, True)
                    chunk(b * CHUNKS + 2 * i + 2, 0, True, True)
            with act.Fori(0, PAIRS - 1) as i:
                chunk(2 * i + ((B - 1) * CHUNKS + 1), 1, True, True)
                chunk(2 * i + ((B - 1) * CHUNKS + 2), 0, True, True)
            chunk(ALL - 1, 1, True, False)
            copy_cols(ALL - 1, TAPS - 1, 1)
            copy_out(ALL - 1, 1)

            act.wait_ge(bn_ready, 1)
            def relu(b):
                for j in range(BANDS):
                    ob = o[:, bass.ds(b * HW + j * BP, BP)]
                    nc.scalar.activation(ob, ob, ACT.Relu, scale=bna[:, 0:1], bias=bna[:, 1:2]).then_inc(relued, 1)

            def normalise(b):
                act.wait_ge(gn_ready, b + (B + 1))
                for h in range(BANDS):
                    first, last = (h * BR + 1 if h else 0), min((h + 1) * BR + 1, H)
                    nc.scalar.activation(interior(xn, b * PW + first + 1, last - first), rows_of(x, b * HW + first * W, (last - first) * W),
                                         ACT.Identity, scale=gn_of(b + B, 0), bias=gn_of(b + B, 1)).then_inc(normed, 1)

            relu(0)
            with act.Fori(0, B - 1) as b:
                normalise(b)
                relu(b + 1)
            normalise(B - 1)

        @block.vector
        def _(dve):
            def rsqrt(n, out, var):
                done = [0]

                def step(ins):
                    done[0] += 1
                    ins.then_inc(rs, 1)
                    dve.wait_ge(rs, n * RSTEPS + done[0])

                v, y, t = rq[:, 0:1], rq[:, 1:2], rq[:, 2:3]
                step(nc.vector.tensor_scalar(v, var, EPS, None, ALU.add))
                step(nc.vector.tensor_scalar(t.bitcast(I32), v.bitcast(I32), 1, None, ALU.arith_shift_right))
                step(nc.vector.tensor_scalar(y.bitcast(I32), t.bitcast(I32), -1.0, float(0x5F3759DF), ALU.mult, ALU.add))
                for i in range(NEWTON):
                    step(nc.vector.tensor_tensor(t, y, y, ALU.mult))
                    step(nc.vector.scalar_tensor_tensor(t, t, -0.5, v, ALU.mult, ALU.mult))
                    step(nc.vector.scalar_tensor_tensor(out if i == NEWTON - 1 else y, t, 1.5, y, ALU.add, ALU.mult))

            def aggregate(s0, slots):
                dve.wait_ge(st, s0)
                alone(dve)
                nc.vector.bn_aggr(mv[:], bst[:, 0:slots].rearrange("p a b -> p (a b)")).then_inc(mvr, 1)

            def group_norm(n, nr, ST):
                dve.wait_ge(gm_done, 2 * n + 1)
                dve.wait_ge(mvr, 2 * n + 1)
                nc.vector.tensor_tensor(dev[:, 0:1], mv[:, 0:1], ST[:, 0:1], ALU.subtract).then_inc(dv, 1)
                dve.wait_ge(dv, n + 1)
                nc.vector.scalar_tensor_tensor(dev[:, 1:2], dev[:, 0:1], dev[:, 0:1], mv[:, 1:2], ALU.mult, ALU.add).then_inc(mvr, 1)
                dve.wait_ge(gm_done, 2 * n + 2)
                rsqrt(nr, gn_of(n, 0), ST[:, 1:2])
                nc.vector.scalar_tensor_tensor(gn_of(n, 1), ST[:, 0:1], -1.0, gn_of(n, 0), ALU.mult, ALU.mult).then_inc(gn_ready, 1)

            def statistics(b):
                s0 = b * CHUNKS
                for j in range(CHUNKS):
                    if isinstance(b, int) and j == CHUNKS // 2:
                        dve.wait_ge(x0b_in, 16)
                    nc.vector.bn_stats(bst[:, j, :], x[:, bass.ds(b * HW + j * CP, CP)]).then_inc(st, 1)
                aggregate(s0 + CHUNKS, CHUNKS)
                group_norm(b, b, ST0)

            def norm_xt(b):
                dve.wait_ge(gn_ready, b + 1)
                nc.vector.tensor_scalar(xt[:].rearrange("p (r w) -> p r w", w=PW)[:, 1:1 + H, 1:1 + W], rows_of(x, b * HW, HW),
                                        gn_of(b, 0), gn_of(b, 1), ALU.mult, ALU.add).then_inc(xt_ready, 1)

            STEPS = 14

            def indices(n, j, par2):
                done = [0]

                def step(ins):
                    done[0] += 1
                    ins.then_inc(ix, 1)
                    dve.wait_ge(ix, n * STEPS + done[0])

                dve.wait_ge(mask_ready, n + 1)
                ot = OT[:, 0:96].rearrange("p (t n) -> p t n", n=32)
                step(nc.vector.tensor_tensor(pos[:], ot[:, :, 0:18], grid[:, j] if isinstance(j, int) else grid[:, bass.ds(j, 1)].rearrange("p a t n -> p (a t) n"), ALU.add))
                step(nc.vector.tensor_scalar(pos[:], pos[:], -1.0, float(H), ALU.max, ALU.min))
                step(nc.vector.tensor_scalar(low[:], pos[:], -0.5, ROUND, ALU.add, ALU.add))
                step(nc.vector.tensor_scalar(low[:], low[:], -ROUND, -1.0, ALU.add, ALU.max))
                step(nc.vector.tensor_scalar(low[:], low[:], float(H - 1), None, ALU.min))
                step(nc.vector.tensor_tensor(frac[:], pos[:], low[:], ALU.subtract))
                step(nc.vector.tensor_scalar(rest[:], frac[:], -1.0, 1.0, ALU.mult, ALU.add))
                step(nc.vector.scalar_tensor_tensor(idxf[:], low[:, :, 0:9], float(PW), low[:, :, 9:18], ALU.mult, ALU.add))
                nc.vector.tensor_scalar(idx[:, par2], idxf[:], float(LEAD + PW + 1), None, ALU.add).then_inc(ix, 1)
                done[0] += 1
                nc.vector.tensor_tensor(my[:, 0], mask[:], rest[:, :, 0:9], ALU.mult).then_inc(ix, 1)
                done[0] += 1
                step(nc.vector.tensor_tensor(my[:, 1], mask[:], frac[:, :, 0:9], ALU.mult))
                for q in range(4):
                    last = nc.vector.tensor_tensor(wt[:, par2, q], my[:, q // 2], (frac if q % 2 else rest)[:, :, 9:18], ALU.mult)
                    if q < 3:
                        last.then_inc(ix, 1)
                        done[0] += 1
                last.then_inc(idx_ready, 1)
                assert done[0] == STEPS

            def out_statistics(c):
                dve.wait_ge(out_copied, c + 3)
                nc.vector.bn_stats(ost[:, bass.ds(c, 1), :].rearrange("p a n -> p (a n)"), o[:, bass.ds(c * CP, CP)]).then_inc(ostat, 1)

            def chunk(c, par2, nj, drain, ahead):
                for k in range(TAPS):
                    dve.wait_ge(gathered[k], c * (16 * TILES) + 16 * TILES)
                    for q in range(1, 4):
                        for t in range(TILES):
                            if q == 1:
                                dve.wait_ge(scaled, c * (TAPS * TILES) + (TAPS * TILES + k * TILES + t + 1))
                            else:
                                dve.wait_ge(lerped, c * (TAPS * LERPS) + (TAPS * LERPS + k * LERPS + (q - 2) * TILES + t + 1))
                            a = acc[:, k % 3, t, :]
                            nc.vector.scalar_tensor_tensor(a, g[:, k, t, q, :], wt[:, par2, q, t, k:k + 1], a,
                                                           ALU.mult, ALU.add).then_inc(lerped, 1)
                    if drain and k == 2:
                        out_statistics(c - 1)
                    if ahead and k == 4:
                        indices(c + 1, nj, 1 - par2)

            dve.wait_ge(x0a_in, 16)
            statistics(0)
            dve.wait_ge(consts, 11)
            norm_xt(0)
            dve.wait_ge(gr_in, 16)
            indices(0, 0, 0)
            dve.wait_ge(xr_in, 16)
            with dve.Fori(1, B) as b:
                statistics(b)
            dve.wait_ge(granted, 1)
            chunk(0, 0, 1, False, True)
            with dve.Fori(0, B - 1) as b:
                dve.wait_ge(tok_turned, (b + 1) * (TT // TG))
                norm_xt(b + 1)
                with dve.Fori(0, PAIRS - 1) as i:
                    chunk(b * CHUNKS + 2 * i + 1, 1, 2 * i + 2, True, True)
                    chunk(b * CHUNKS + 2 * i + 2, 0, 2 * i + 3, True, True)
                chunk(b * CHUNKS + (CHUNKS - 1), 1, 0, True, True)
                chunk(b * CHUNKS + CHUNKS, 0, 1, True, True)
            with dve.Fori(0, PAIRS - 1) as i:
                chunk(2 * i + ((B - 1) * CHUNKS + 1), 1, 2 * i + 2, True, True)
                chunk(2 * i + ((B - 1) * CHUNKS + 2), 0, 2 * i + 3, True, True)
            dve.wait_ge(w1_in, 16)
            nc.vector.tensor_scalar(w_outer, w1_rows[:, :, 0], 0.5, None, ALU.mult).then_inc(w_mixed, 1)
            dve.wait_ge(w_mixed, 1)
            nc.vector.scalar_tensor_tensor(w_outer, w1_rows[:, :, 2], 0.5, w_outer, ALU.mult, ALU.add).then_inc(w_mixed, 1)
            dve.wait_ge(w_mixed, 2)
            nc.vector.scalar_tensor_tensor(w_plus, w1_rows[:, :, 1], 0.5, w_outer, ALU.mult, ALU.add).then_inc(w_mixed, 1)
            nc.vector.scalar_tensor_tensor(w_minus, w1_rows[:, :, 1], -0.5, w_outer, ALU.mult, ALU.add).then_inc(w_mixed, 1)
            chunk(ALL - 1, 1, None, True, False)
            out_statistics(ALL - 1)

            dve.wait_ge(ostat, ALL)
            dve.wait_ge(wc_in, 32)
            nc.vector.bn_aggr(omv[:], ost[:].rearrange("p a b -> p (a b)")).then_inc(ostat, 1)
            dve.wait_ge(ostat, ALL + 1)
            rsqrt(B, bna[:, 2:3], omv[:, 1:2])
            dve.wait_ge(rs, (B + 1) * RSTEPS)
            nc.vector.tensor_tensor(bna[:, 0:1], bna[:, 2:3], par[:, 1:2], ALU.mult).then_inc(ostat, 1)
            dve.wait_ge(ostat, ALL + 2)
            nc.vector.tensor_tensor(bna[:, 2:3], omv[:, 0:1], bna[:, 0:1], ALU.mult).then_inc(ostat, 1)
            dve.wait_ge(ostat, ALL + 3)
            nc.vector.tensor_tensor(bna[:, 1:2], par[:, 2:3], bna[:, 2:3], ALU.subtract).then_inc(bn_ready, 1)

            def sums(b):
                for j in range(BANDS):
                    dve.wait_ge(added, b * BANDS + (j + 1))
                    for i in range(2):
                        nc.vector.bn_stats(bst[:, 2 * j + i, :], x[:, bass.ds(b * HW + j * BP + i * HB, HB)]).then_inc(st, 1)
                aggregate(b * (2 * BANDS) + (B * CHUNKS + 2 * BANDS), 2 * BANDS)

            def finish(n, h):
                pairs = x[:, bass.ds(n * BP, BP)].rearrange("p (i two) -> p i two", two=2)
                even, odd = pairs[:, :, 0], pairs[:, :, 1]
                m0, m1, m2, m3 = (t[:, 0:HB] for t in MX[h % 2])
                s = n * 4
                dve.wait_ge(conv1, MIX * n + (2 + MIX * BANDS))
                nc.vector.scalar_tensor_tensor(even, m1, par[:, 3:4], even, ALU.add, ALU.add).then_inc(unmixed, 1)
                nc.vector.scalar_tensor_tensor(odd, m1, par[:, 3:4], odd, ALU.add, ALU.add).then_inc(unmixed, 1)
                dve.wait_ge(unmixed, s + 1)
                nc.vector.tensor_tensor(even, even, m0, ALU.add).then_inc(unmixed, 1)
                dve.wait_ge(conv1, MIX * n + (3 + MIX * BANDS))
                dve.wait_ge(unmixed, s + 2)
                nc.vector.tensor_tensor(odd, odd, m2, ALU.subtract).then_inc(unmixed, 1)
                dve.wait_ge(unmixed, s + 3)
                nc.vector.tensor_tensor(even, even, m2, ALU.add).then_inc(fin, 1)
                dve.wait_ge(conv1, MIX * n + (4 + MIX * BANDS))
                dve.wait_ge(unmixed, s + 4)
                nc.vector.tensor_tensor(odd, odd, m3, ALU.subtract).then_inc(fin, 1)

            sums(0)
            group_norm(B, B + 1, ST1)
            dve.wait_ge(normed, 1)
            for m in range(MIX):
                mix(nc.vector, 0, 0, m).then_inc(mixed0, 1)
            with dve.Fori(0, B - 1) as b:
                finish(b * BANDS, 0)
                sums(b + 1)
                finish(b * BANDS + 1, 1)
                group_norm(b + (B + 1), b + (B + 2), ST1)
                finish(b * BANDS + 2, 2)
                finish(b * BANDS + 3, 3)
            for h in range(BANDS):
                finish((B - 1) * BANDS + h, h)


_LAYOUT = "weights with input channels first; offsets as 9 dy, 9 dx, 9 mask rows"


def kernel(x, L0_conv_w_offset, L0_conv_b_offset, L0_conv_w_conv, L0_conv_b_conv, L0_conv_gamma, L0_conv_beta,
           L1_conv_weight, L1_conv_bias):
    import numpy as np
    import concourse.bacc as bacc
    from concourse.bass_utils import run_bass_kernel_spmd as run

    def taps_first(w):
        return np.ascontiguousarray(np.transpose(w, (1, 2, 3, 0))).reshape(P, TAPS, w.shape[0])

    order = [2 * k for k in range(9)] + [2 * k + 1 for k in range(9)] + list(range(18, 27))
    n = np.arange(HW).reshape(CHUNKS * TILES, P).T
    k = np.arange(TAPS)
    gy = (n // W)[:, :, None] + (k // 3 - 1)[None, None, :]
    gx = (n % W)[:, :, None] + (k % 3 - 1)[None, None, :]
    grid = np.concatenate([gy, gx], axis=2).astype(np.float32).reshape(P, CHUNKS, TILES, 18)
    arrays = {
        "x_dram": np.ascontiguousarray(np.transpose(np.asarray(x), (1, 0, 2, 3))).reshape(P, B, HW),
        "woff_dram": taps_first(np.asarray(L0_conv_w_offset)[order]),
        "wconv_dram": taps_first(np.asarray(L0_conv_w_conv)),
        "w1_dram": taps_first(np.asarray(L1_conv_weight)),
        "boff_dram": np.ascontiguousarray(np.asarray(L0_conv_b_offset)[order]).reshape(27, 1),
        "par_dram": np.ascontiguousarray(np.stack([np.asarray(v) for v in (
            L0_conv_b_conv, L0_conv_gamma, L0_conv_beta, L1_conv_bias, L1_conv_bias)], axis=1)),
        "grid_dram": grid,
    }
    nc = bacc.Bacc("TRN2", target_bir_lowering=False, num_devices=1)
    aps = [nc.dram_tensor(name, a.shape, F32, kind="ExternalInput").ap() for name, a in arrays.items()]
    out = nc.dram_tensor("out_dram", (P, B * HW), F32, kind="ExternalOutput").ap()
    build(nc, *aps, out)
    r = run(nc, [arrays], core_ids=[0])
    y = r.results[0]["out_dram"].reshape(P, B, H, W)
    return np.ascontiguousarray(np.transpose(y, (1, 0, 2, 3)))
```

```python
import concourse.bass as bass
from concourse import mybir
from contextlib import ExitStack

F32 = mybir.dt.float32
I32 = mybir.dt.int32
ALU = mybir.AluOpType
ACT = mybir.ActivationFunctionType

P = 128
B, H, W = 4, 48, 48
HW = H * W
TAPS = 9
PW = W + 2
TILES = 3
CP = TILES * P
ROWS = CP // W
CHUNKS = HW // CP
PAIRS = CHUNKS // 2
ALL = B * CHUNKS
GROUP = 4
EPS = 1e-5
TT = 20
TG = 4
TURN_TAPS = [(3, 6), (3, 8), (4, 4), (4, 6), (4, 8)]
COPY_TAPS = [(3, 8), (4, 1), (4, 6), (4, 8), (5, 1)]
LEAD = 64
BANKS = TT // TG
TABLE = LEAD + TT * P
ROUND = 12582912.0
NEWTON = 3
RSTEPS = 4 + 2 * NEWTON
LERPS = 3 * TILES
BANDS = 4
BR = H // BANDS
BP = BR * W
HB = BP // 2
HALF = W // 2
BAND_ORDER = (1, 0, 3, 2)
MIX = 4


def build(nc, x_d, woff_d, wconv_d, w1_d, boff_d, par_d, grid_d, out_d):
    tables = [nc.dram_tensor(f"corner_table{b}", [TABLE, 4 * P], F32, kind="Internal").ap() for b in range(B)]

    with ExitStack() as ctx:
        def sb(name, shape, dt=F32):
            return ctx.enter_context(nc.sbuf_tensor(name, shape, dt))

        def ps(name):
            return ctx.enter_context(nc.psum_tensor(name, [P, 512], F32))

        def sem(name):
            return ctx.enter_context(nc.semaphore(name))

        x = sb("x", [P, B * HW])
        o = sb("o", [P, B * HW])
        xn = sb("xn", [P, B * PW, PW])
        xt = sb("xt", [P, 52 * PW])
        tok = sb("tok", [P, TT, P])
        g = sb("g", [P, TAPS, TILES, 4, P])
        mixed = g[:].rearrange("p k t q c -> p (k t q c)")[:, 0:MIX * PW * HALF].rearrange("p (m r w) -> p m r w", m=MIX, w=HALF)
        acc = sb("acc", [P, 3, TILES, P])
        cols = sb("cols", [P, 2, CP])
        woff = sb("woff", [P, TAPS, 27])
        wconv = sb("wconv", [P, TAPS, P])
        w1 = tok[:, 0:TAPS, :]
        w1_rows = w1.rearrange("p (y x) c -> p y x c", x=3)
        w_plus, w_minus, w_outer = (tok[:, TAPS + i:TAPS + i + 3, :] for i in (0, 3, 6))
        boff = sb("boff", [27, 1])
        params = sb("params", [P, 4])
        grid = sb("grid", [P, CHUNKS, TILES, 18])
        ident = sb("ident", [P, P])
        gavg = sb("gavg", [P, P])
        om = sb("om", [27, CP])
        mask = sb("mask", [P, TILES, 9])
        pos = sb("pos", [P, TILES, 18])
        low = sb("low", [P, TILES, 18])
        frac = sb("frac", [P, TILES, 18])
        rest = sb("rest", [P, TILES, 18])
        my = sb("my", [P, 2, TILES, 9])
        idxf = sb("idxf", [P, TILES, 9])
        idx = sb("idx", [P, 2, TILES, 9], I32)
        wt = sb("wt", [P, 2, 4, TILES, 9])
        bst = sb("bst", [P, 2 * BANDS, 6])
        mv = sb("mv", [P, 2])
        dev = sb("dev", [P, 2])
        gn = sb("gn", [P, 2 * B, 2])
        ost = sb("ost", [P, ALL, 6])
        omv = sb("omv", [P, 2])
        rq = sb("rq", [P, 4])
        bna = sb("bna", [P, 4])

        OM = ps("OM")
        OT = ps("OT")
        TP = (ps("TP0"), ps("TP1"))
        CO = (ps("CO0"), ps("CO1"))
        PT = (ps("PT0"), ps("PT1"))
        ST0, ST1 = OT[:, 500:502], OM[:, 500:502]
        MX = ((OM, OT, *TP), (*CO, *PT))

        x0a_in, x0b_in = sem("x0a_in"), sem("x0b_in")
        xr_in = sem("xr_in")
        wo_in = sem("wo_in")
        gr_in = sem("gr_in")
        wc_in = sem("wc_in")
        w1_in = sem("w1_in")
        consts = sem("consts")
        stats_in = sem("stats_in")
        dev_ready = sem("dev_ready")
        group_sums = sem("group_sums")
        gn_ready = sem("gn_ready")
        group_terms = sem("group_terms")
        xt_ready = sem("xt_ready")
        xn_ready = sem("xn_ready")
        tok_turned = sem("tok_turned")
        tok_ready = sem("tok_ready")
        ends = sem("ends")
        tabled = sem("tabled")
        om_ready = sem("om_ready")
        om_copied = sem("om_copied")
        om_turned = sem("om_turned")
        mask_ready = sem("mask_ready")
        idx_ready = sem("idx_ready")
        gathered = [sem(f"gathered{k}") for k in range(TAPS)]
        scaled = sem("scaled")
        lerped = sem("lerped")
        turned = sem("turned")
        copied = sem("copied")
        conved = sem("conved")
        out_copied = sem("out_copied")
        granted = sem("granted")
        passed = sem("passed")
        index_step = sem("index_step")
        rsqrt_step = sem("rsqrt_step")
        bn_terms = sem("bn_terms")
        warm = sem("warm")
        bn_ready = sem("bn_ready")
        w_mixed = sem("w_mixed")
        relued = sem("relued")
        added = sem("added")
        summed = sem("summed")
        normed = sem("normed")
        mixed0 = sem("mixed0")
        mixed_ready = sem("mixed_ready")
        conv1 = sem("conv1")
        unmixed = sem("unmixed")
        finished = sem("finished")
        stored = sem("stored")

        block = ctx.enter_context(nc.Block())

        def interior(t, row, rows):
            return t[:, bass.ds(row, rows), 1:1 + W]

        def gn_of(n, i):
            return gn[:, bass.ds(n, 1), i]

        def rows_of(t, start, n):
            return t[:, bass.ds(start, n)].rearrange("p (r w) -> p r w", w=W)

        def add_band(eng, b, j):
            xs = x[:, bass.ds(b * HW + j * BP, BP)]
            return eng.tensor_tensor(xs, xs, o[:, bass.ds(b * HW + j * BP, BP)], ALU.add)

        def mix(eng, b, h, m):
            first, rows = (0, BR + 2) if h == 0 else (h * BR + 2, BR)
            src = xn[:, bass.ds(b * PW + first, rows), :]
            d0, d2 = src[:, :, 0:W:2], src[:, :, 2:PW:2]
            d1, d3 = src[:, :, 1:W:2], src[:, :, 3:PW:2]
            p, q, op = ((d0, d2, ALU.subtract), (d1, d2, ALU.add), (d2, d1, ALU.subtract), (d1, d3, ALU.subtract))[m]
            return eng.tensor_tensor(mixed[:, m, first:first + rows, :], p, q, op)

        def alone(eng):
            eng.sem_inc(passed, 1)

        @block.sync
        def _(sp):
            sp.sem_inc(scaled, TAPS * TILES)
            sp.sem_inc(lerped, TAPS * LERPS)
            sp.sem_inc(turned, TAPS)
            sp.sem_inc(copied, TAPS)
            sp.sem_inc(conved, TAPS)
            sp.sem_inc(out_copied, 2)
            sp.sem_inc(finished, 4)
            sp.sem_inc(conv1, MIX * BANDS)
            sp.sem_inc(granted, 1)
            sp.dma_start(x[:, 0:HW // 2], x_d[:, 0, 0:HW // 2]).then_inc(x0a_in, 16)
            sp.dma_start(x[:, HW // 2:HW], x_d[:, 0, HW // 2:]).then_inc(x0b_in, 16)
            sp.dma_start(woff[:], woff_d).then_inc(wo_in, 16)
            sp.dma_start(boff[:], boff_d).then_inc(wo_in, 16)
            sp.dma_start(grid[:], grid_d).then_inc(gr_in, 16)
            zeros = acc[0:LEAD].rearrange("p a t c -> p (a t c)")[:, 0:4 * P]

            def load_image(b):
                sp.dma_start(x[:, b * HW:(b + 1) * HW], x_d[:, b]).then_inc(xr_in, 16)

            def clear_ends(b):
                sp.dma_start(tables[b][0:LEAD], zeros).then_inc(ends, 16)
                sp.dma_start(tables[b][TABLE - LEAD:TABLE], zeros).then_inc(ends, 16)

            def write_table(b):
                for j in range(BANKS):
                    sp.wait_ge(tok_ready, b * BANKS + (j + 1))
                    for q in range(4):
                        shift = PW * (q // 2) + q % 2
                        row = LEAD + j * TG * P - shift
                        dst = tables[b][row:row + TG * P, q * P:(q + 1) * P]
                        sp.dma_start(dst.rearrange("(t p) c -> p t c", p=P), tok[:, j * TG:(j + 1) * TG, :]).then_inc(tabled, 16)
                    if 0 < b < B - 1 and j == 1:
                        load_image(b + 1)
                if b == 0:
                    sp.dma_start(wconv[:], wconv_d).then_inc(wc_in, 16)
                    sp.dma_start(params[:], par_d).then_inc(wc_in, 16)

            sp.wait_ge(consts, 6)
            for b in range(B):
                clear_ends(b)
            load_image(1)
            sp.wait_ge(ends, 2 * B * 16)
            for b in range(B):
                write_table(b)
            sp.wait_ge(tabled, B * 16 * TT)
            sp.dma_start(w1, w1_d).then_inc(w1_in, 16)
            with sp.Fori(0, B * BANDS) as i:
                sp.wait_ge(finished, 2 * i + 6)
                sp.dma_start(out_d[:, bass.ds(i * BP, BP)], x[:, bass.ds(i * BP, BP)]).then_inc(stored, 16)
            sp.wait_ge(stored, 16 * B * BANDS)

        @block.gpsimd
        def _(pl):
            xn4 = xn[:].rearrange("p (b r) w -> p b r w", b=B)
            xt3 = xt[:].rearrange("p (r w) -> p r w", w=PW)
            pl.memset(xt3[:, 0:1], 0.0).then_inc(consts, 1)
            pl.memset(xt3[:, 1 + H:], 0.0).then_inc(consts, 1)
            pl.memset(xt3[:, 1:1 + H, 0:PW:PW - 1], 0.0).then_inc(consts, 1)
            pl.memset(xn4[:, :, 0:PW:PW - 1, :], 0.0).then_inc(consts, 1)
            pl.memset(xn4[:, :, 1:1 + H, 0:PW:PW - 1], 0.0).then_inc(consts, 1)
            pl.memset(acc[:], 0.0).then_inc(consts, 1)
            pl.memset(ident[:], 0.0).then_inc(consts, 1)
            pl.memset(gavg[:], 1.0 / GROUP).then_inc(consts, 1)
            pl.wait_ge(consts, 8)
            pl.affine_select(out=ident[:], in_=ident[:], compare_op=ALU.not_equal, fill=1.0, base=0,
                             pattern=[[-1, P]], channel_multiplier=1).then_inc(consts, 1)
            gv = gavg[:].rearrange("p (a b) -> p a b", b=GROUP)
            pl.affine_select(out=gv, in_=gv, compare_op=ALU.is_ge, fill=0.0, base=0,
                             pattern=[[-GROUP, P // GROUP], [0, GROUP]], channel_multiplier=1).then_inc(consts, 1)
            pl.wait_ge(consts, 10)
            pl.affine_select(out=gv, in_=gv, compare_op=ALU.is_ge, fill=0.0, base=GROUP - 1,
                             pattern=[[GROUP, P // GROUP], [0, GROUP]], channel_multiplier=-1).then_inc(consts, 1)

            for b in range(B):
                pl.wait_ge(tabled, (b + 1) * (16 * TT))
                with pl.Fori(0, PAIRS) as i:
                    for parity in range(2):
                        c = 2 * i + (b * CHUNKS + parity)
                        pl.wait_ge(idx_ready, c + 1)
                        for k in range(TAPS):
                            pl.wait_ge(lerped, c * (TAPS * LERPS) + (k + 1) * LERPS)
                            alone(pl)
                            for t in range(TILES):
                                pl.indirect_dma_start(
                                    out=g[:, k, t].rearrange("p q c -> p (q c)"), out_offset=None, in_=tables[b],
                                    in_offset=bass.IndirectOffsetOnAxis(ap=idx[:, parity, t, k:k + 1], axis=0),
                                ).then_inc(gathered[k], 16)

            def add(b):
                for j in range(0, BANDS, 2):
                    pl.wait_ge(relued, b * BANDS + (BAND_ORDER.index(j) + 1))
                    add_band(pl, b, j).then_inc(added, 1)

            def mix_band(b, h):
                pl.wait_ge(normed, b * BANDS + (h + 1))
                pl.wait_ge(conv1, MIX * (b * BANDS + min(h + 2, BANDS)))
                for m in range(MIX):
                    mix(pl, b, h, m).then_inc(mixed_ready, 1)

            add(0)
            with pl.Fori(0, B - 1) as b:
                mix_band(b, 1)
                mix_band(b, 2)
                add(b + 1)
                mix_band(b, 3)
                mix_band(b + 1, 0)
            for h in range(1, BANDS):
                mix_band(B - 1, h)

        @block.tensor
        def _(pe):
            def group_mean(n, ST):
                pe.wait_ge(group_terms, 2 * n + 1)
                nc.tensor.matmul(ST[:, 0:1], gavg[:], mv[:, 0:1], start=True, stop=True).then_inc(group_sums, 1)

            def group_var(n, ST):
                pe.wait_ge(group_terms, 2 * n + 2)
                nc.tensor.matmul(ST[:, 1:2], gavg[:], dev[:, 1:2], start=True, stop=True).then_inc(group_sums, 1)

            def turn_bank(b, j):
                pe.wait_ge(xt_ready, b * BANKS + (j + 1))
                if j >= 2:
                    pe.wait_ge(tok_ready, b * BANKS + (j - 1))
                for t in range(TG):
                    n = (j * TG + t) * P
                    last = nc.tensor.transpose(PT[j % 2][:, t * P:(t + 1) * P], xt[:, n:n + P], ident[:])
                last.then_inc(tok_turned, 1)

            def prepare(b, j, k):
                if (j, k) == (1, 6):
                    group_mean(b, ST0)
                if (j, k) == (2, 6):
                    group_var(b, ST0)
                if (j, k) in TURN_TAPS:
                    turn_bank(b, TURN_TAPS.index((j, k)))

            def offset_conv(row, taps=range(TAPS)):
                for k in taps:
                    last = nc.tensor.matmul(OM[0:27, 0:CP], woff[:, k, :],
                                            xn[:, bass.ds(row + k // 3, ROWS), k % 3:k % 3 + W],
                                            start=(k == 0), stop=(k == TAPS - 1))
                if taps[-1] == TAPS - 1:
                    last.then_inc(om_ready, 1)

            def turn_offsets(n):
                pe.wait_ge(om_copied, n + 1)
                alone(pe)
                for t in range(TILES):
                    last = nc.tensor.transpose(OT[:, 32 * t:32 * t + 27], om[:, t * P:(t + 1) * P], ident[0:27, 0:27])
                last.then_inc(om_turned, 1)

            def conv_tap(c, k, parity):
                pe.wait_ge(copied, c * TAPS + (TAPS + k + 1))
                nc.tensor.matmul(CO[parity][:, 0:CP], wconv[:, k, :], cols[:, (parity + k) % 2, :],
                                 start=(k == 0), stop=(k == TAPS - 1)).then_inc(conved, 1)

            def chunk(c, parity, row, drain, ahead, prep=None):
                for k in range(TAPS):
                    if ahead and k < 3:
                        offset_conv(row, range(3 * k, 3 * k + 3))
                    if drain and k == 0:
                        conv_tap(c - 1, TAPS - 1, 1 - parity)
                    if k == TAPS - 1 and not ahead:
                        conv_tap(c, k - 1, parity)
                    pe.wait_ge(lerped, c * (TAPS * LERPS) + (TAPS * LERPS + (k + 1) * LERPS))
                    pe.wait_ge(copied, c * TAPS + (TAPS + k - 1))
                    for t in range(TILES):
                        last = nc.tensor.transpose(TP[(parity + k) % 2][:, t * P:(t + 1) * P], acc[:, k % 3, t, :], ident[:])
                    last.then_inc(turned, 1)
                    if k == 1:
                        pe.wait_ge(out_copied, c + 1)
                    if k and (k < TAPS - 1 or ahead):
                        conv_tap(c, k - 1, parity)
                    if ahead and k == 3:
                        turn_offsets(c + 1)
                    if prep is not None:
                        prepare(*prep, k)

            pe.wait_ge(consts, 11)
            group_mean(0, ST0)
            group_var(0, ST0)
            for j in range(BANKS):
                turn_bank(0, j)
            pe.wait_ge(wo_in, 32)
            pe.wait_ge(xn_ready, 1)
            offset_conv(0)
            turn_offsets(0)
            pe.wait_ge(wc_in, 32)
            pe.wait_ge(granted, 1)
            pe.wait_ge(xn_ready, 2)
            chunk(0, 0, ROWS, False, True)
            with pe.Fori(0, B - 1) as b:
                for j in range(1, CHUNKS + 1):
                    if j == CHUNKS - 1:
                        pe.wait_ge(xn_ready, 2 * b + 4)
                        alone(pe)
                    row = b * PW + (j + 1) * ROWS if j + 1 < CHUNKS else (b + 1) * PW + (j + 1 - CHUNKS) * ROWS
                    chunk(b * CHUNKS + j, j % 2, row, True, True, (b + 1, j))
            with pe.Fori(0, PAIRS - 1) as i:
                c = 2 * i + (B - 1) * CHUNKS
                chunk(c + 1, 1, i * (2 * ROWS) + ((B - 1) * PW + 2 * ROWS), True, True)
                chunk(c + 2, 0, i * (2 * ROWS) + ((B - 1) * PW + 3 * ROWS), True, True)
            chunk(ALL - 1, 1, None, True, False)
            conv_tap(ALL - 1, TAPS - 1, 1)

            def layer1_band(n, h, first, stats=None):
                pe.wait_ge(finished, 2 * n + 2)
                for m in range(MIX):
                    if first:
                        pe.wait_ge(mixed0, m + 1)
                    else:
                        pe.wait_ge(mixed_ready, MIX * n + (m + 1 - MIX))
                    for ky in range(3):
                        w = (w1_rows[:, ky, 0], w_plus[:, ky], w_minus[:, ky], w1_rows[:, ky, 2])[m]
                        r = h * BR + ky
                        last = nc.tensor.matmul(MX[h % 2][m][:, 0:HB], w, mixed[:, m, r:r + BR, :], start=(ky == 0), stop=(ky == 2))
                    last.then_inc(conv1, 1)
                    if stats is not None and m == 0:
                        group_mean(stats, ST1)
                    if stats is not None and m == 2:
                        group_var(stats, ST1)

            pe.wait_ge(w_mixed, 4)
            group_mean(B, ST1)
            group_var(B, ST1)
            layer1_band(0, 0, True)
            with pe.Fori(0, B - 1) as b:
                layer1_band(b * BANDS + 1, 1, False)
                layer1_band(b * BANDS + 2, 2, False, b + (B + 1))
                layer1_band(b * BANDS + 3, 3, False)
                layer1_band(b * BANDS + 4, 0, False)
            for h in range(1, BANDS):
                layer1_band((B - 1) * BANDS + h, h, False)

        @block.scalar
        def _(act):
            def norm_xn(b, part):
                first, last = ((0, ROWS + 1), (ROWS + 1, H))[part]
                act.wait_ge(gn_ready, b + 1)
                nc.scalar.activation(interior(xn, b * PW + 1 + first, last - first), rows_of(x, b * HW + first * W, (last - first) * W),
                                     ACT.Identity, scale=gn_of(b, 0), bias=gn_of(b, 1)).then_inc(xn_ready, 1)

            def copy_bank(b, j):
                act.wait_ge(tok_turned, b * BANKS + (j + 1))
                nc.scalar.activation(tok[:, j * TG:(j + 1) * TG, :].rearrange("p t c -> p (t c)"), PT[j % 2][:], ACT.Copy).then_inc(tok_ready, 1)

            def prepare(b, j, k):
                if (j, k) == (3, 5):
                    norm_xn(b, 0)
                    norm_xn(b, 1)
                if (j, k) in COPY_TAPS:
                    i = COPY_TAPS.index((j, k))
                    if i == 0:
                        act.wait_ge(tabled, b * (16 * TT))
                    copy_bank(b, i)

            def copy_offsets(n):
                act.wait_ge(om_ready, n + 1)
                nc.scalar.activation(om[:], OM[0:27, 0:CP], ACT.Identity, bias=boff[:]).then_inc(om_copied, 1)

            def masks(n):
                act.wait_ge(om_turned, n + 1)
                nc.scalar.activation(mask[:], OT[:, 0:96].rearrange("p (t n) -> p t n", n=32)[:, :, 18:27], ACT.Sigmoid).then_inc(mask_ready, 1)

            def copy_cols(c, k, parity):
                act.wait_ge(turned, c * TAPS + (TAPS + k + 1))
                act.wait_ge(conved, c * TAPS + (TAPS + k - 1))
                nc.scalar.activation(cols[:, (parity + k) % 2, :], TP[(parity + k) % 2][:, 0:CP], ACT.Copy).then_inc(copied, 1)

            def copy_out(c, parity):
                act.wait_ge(conved, c * TAPS + 2 * TAPS)
                nc.scalar.activation(o[:, bass.ds(c * CP, CP)], CO[parity][:, 0:CP], ACT.Identity, bias=params[:, 0:1]).then_inc(out_copied, 1)

            def chunk(c, parity, drain, ahead, prep=None):
                act.wait_ge(idx_ready, c + 1)
                for k in range(TAPS):
                    act.wait_ge(gathered[k], c * (16 * TILES) + 16 * TILES)
                    act.wait_ge(turned, c * TAPS + (TAPS + k - 2))
                    for t in range(TILES):
                        nc.scalar.activation(acc[:, k % 3, t, :], g[:, k, t, 0, :], ACT.Copy,
                                             scale=wt[:, parity, 0, t, k:k + 1]).then_inc(scaled, 1)
                    if drain and k == 0:
                        copy_cols(c - 1, TAPS - 1, 1 - parity)
                    if drain and k == 1:
                        copy_out(c - 1, 1 - parity)
                    if k:
                        copy_cols(c, k - 1, parity)
                    if ahead and k == 3:
                        copy_offsets(c + 1)
                    if ahead and k == 4:
                        masks(c + 1)
                    if prep is not None:
                        prepare(*prep, k)

            act.wait_ge(consts, 11)
            nc.scalar.activation(mask[:], acc[:, 0, :, 0:9], ACT.Sigmoid).then_inc(warm, 1)
            act.wait_ge(x0b_in, 16)
            norm_xn(0, 0)
            for j in range(BANKS):
                copy_bank(0, j)
            norm_xn(0, 1)
            act.wait_ge(wo_in, 32)
            copy_offsets(0)
            masks(0)
            act.wait_ge(granted, 1)
            act.wait_ge(wc_in, 32)
            chunk(0, 0, False, True)
            with act.Fori(0, B - 1) as b:
                for j in range(1, CHUNKS + 1):
                    chunk(b * CHUNKS + j, j % 2, True, True, (b + 1, j))
            with act.Fori(0, PAIRS - 1) as i:
                chunk(2 * i + ((B - 1) * CHUNKS + 1), 1, True, True)
                chunk(2 * i + ((B - 1) * CHUNKS + 2), 0, True, True)
            chunk(ALL - 1, 1, True, False)
            copy_cols(ALL - 1, TAPS - 1, 1)
            copy_out(ALL - 1, 1)

            def relu(b):
                for j in BAND_ORDER:
                    ob = o[:, bass.ds(b * HW + j * BP, BP)]
                    nc.scalar.activation(ob, ob, ACT.Relu, scale=bna[:, 0:1], bias=bna[:, 1:2]).then_inc(relued, 1)

            def normalise(b):
                act.wait_ge(gn_ready, b + (B + 1))
                for h in range(BANDS):
                    first, last = (h * BR + 1 if h else 0), min((h + 1) * BR + 1, H)
                    nc.scalar.activation(interior(xn, b * PW + first + 1, last - first), rows_of(x, b * HW + first * W, (last - first) * W),
                                         ACT.Identity, scale=gn_of(b + B, 0), bias=gn_of(b + B, 1)).then_inc(normed, 1)

            act.wait_ge(bn_ready, 1)
            relu(0)
            normalise(0)
            with act.Fori(1, B) as b:
                relu(b)
                normalise(b)

        @block.vector
        def _(dve):
            def rsqrt(n, out, var):
                done = [0]

                def step(ins):
                    done[0] += 1
                    ins.then_inc(rsqrt_step, 1)
                    dve.wait_ge(rsqrt_step, n * RSTEPS + done[0])

                v, y, t, nv = (rq[:, i:i + 1] for i in range(4))
                nc.vector.tensor_scalar(nv, var, EPS, -0.5, ALU.add, ALU.mult).then_inc(rsqrt_step, 1)
                done[0] += 1
                step(nc.vector.tensor_scalar(v, var, EPS, None, ALU.add))
                step(nc.vector.tensor_scalar(t.bitcast(I32), v.bitcast(I32), 1, None, ALU.arith_shift_right))
                step(nc.vector.tensor_scalar(y.bitcast(I32), t.bitcast(I32), -1.0, float(0x5F3759DF), ALU.mult, ALU.add))
                for i in range(NEWTON):
                    step(nc.vector.tensor_scalar(t, y, y, nv, ALU.mult, ALU.mult))
                    step(nc.vector.scalar_tensor_tensor(out if i == NEWTON - 1 else y, t, 1.5, y, ALU.add, ALU.mult))

            def aggregate(s0, slots):
                dve.wait_ge(stats_in, s0)
                alone(dve)
                nc.vector.bn_aggr(mv[:], bst[:, 0:slots].rearrange("p a b -> p (a b)")).then_inc(group_terms, 1)

            def group_norm(n, nr, ST):
                deviation(n, ST)
                group_scale(n, nr, ST)

            def deviation(n, ST):
                dve.wait_ge(group_sums, 2 * n + 1)
                dve.wait_ge(group_terms, 2 * n + 1)
                nc.vector.tensor_tensor(dev[:, 0:1], mv[:, 0:1], ST[:, 0:1], ALU.subtract).then_inc(dev_ready, 1)
                dve.wait_ge(dev_ready, n + 1)
                nc.vector.scalar_tensor_tensor(dev[:, 1:2], dev[:, 0:1], dev[:, 0:1], mv[:, 1:2], ALU.mult, ALU.add).then_inc(group_terms, 1)

            def group_scale(n, nr, ST):
                dve.wait_ge(group_sums, 2 * n + 2)
                rsqrt(nr, gn_of(n, 0), ST[:, 1:2])
                nc.vector.scalar_tensor_tensor(gn_of(n, 1), ST[:, 0:1], -1.0, gn_of(n, 0), ALU.mult, ALU.mult).then_inc(gn_ready, 1)

            def statistics(b):
                s0 = b * CHUNKS
                for j in range(CHUNKS):
                    if isinstance(b, int) and j == CHUNKS // 2:
                        dve.wait_ge(x0b_in, 16)
                    nc.vector.bn_stats(bst[:, j, :], x[:, bass.ds(b * HW + j * CP, CP)]).then_inc(stats_in, 1)
                aggregate(s0 + CHUNKS, CHUNKS)

            def norm_xt(b):
                dve.wait_ge(gn_ready, b + 1)
                first = 0
                for j in range(BANKS):
                    last = min((j + 1) * TG * P // PW, H)
                    nc.vector.tensor_scalar(xt[:].rearrange("p (r w) -> p r w", w=PW)[:, 1 + first:1 + last, 1:1 + W],
                                            rows_of(x, b * HW + first * W, (last - first) * W),
                                            gn_of(b, 0), gn_of(b, 1), ALU.mult, ALU.add).then_inc(xt_ready, 1)
                    first = last

            def prepare(b, j, k):
                if (j, k) == (1, 5):
                    dve.wait_ge(xr_in, b * 16)
                    alone(dve)
                    statistics(b)
                if (j, k) == (2, 5):
                    deviation(b, ST0)
                if (j, k) == (2, 7):
                    group_scale(b, b, ST0)
                if (j, k) == (3, 5):
                    dve.wait_ge(tok_turned, b * BANKS)
                    norm_xt(b)

            STEPS = 14

            def indices(n, j, parity):
                done = [0]

                def step(ins):
                    done[0] += 1
                    ins.then_inc(index_step, 1)
                    dve.wait_ge(index_step, n * STEPS + done[0])

                dve.wait_ge(mask_ready, n + 1)
                ot = OT[:, 0:96].rearrange("p (t n) -> p t n", n=32)
                step(nc.vector.tensor_tensor(pos[:], ot[:, :, 0:18], grid[:, bass.ds(j, 1)].rearrange("p a t n -> p (a t) n"), ALU.add))
                step(nc.vector.tensor_scalar(pos[:], pos[:], -1.0, float(H), ALU.max, ALU.min))
                step(nc.vector.tensor_scalar(low[:], pos[:], -0.5, ROUND, ALU.add, ALU.add))
                step(nc.vector.tensor_scalar(low[:], low[:], -ROUND, -1.0, ALU.add, ALU.max))
                step(nc.vector.tensor_scalar(low[:], low[:], float(H - 1), None, ALU.min))
                step(nc.vector.tensor_tensor(frac[:], pos[:], low[:], ALU.subtract))
                step(nc.vector.tensor_scalar(rest[:], frac[:], -1.0, 1.0, ALU.mult, ALU.add))
                step(nc.vector.scalar_tensor_tensor(idxf[:], low[:, :, 0:9], float(PW), low[:, :, 9:18], ALU.mult, ALU.add))
                nc.vector.tensor_scalar(idx[:, parity], idxf[:], float(LEAD + PW + 1), None, ALU.add).then_inc(index_step, 1)
                done[0] += 1
                nc.vector.tensor_tensor(my[:, 0], mask[:], rest[:, :, 0:9], ALU.mult).then_inc(index_step, 1)
                done[0] += 1
                step(nc.vector.tensor_tensor(my[:, 1], mask[:], frac[:, :, 0:9], ALU.mult))
                for q in range(4):
                    last = nc.vector.tensor_tensor(wt[:, parity, q], my[:, q // 2], (frac if q % 2 else rest)[:, :, 9:18], ALU.mult)
                    if q < 3:
                        last.then_inc(index_step, 1)
                        done[0] += 1
                last.then_inc(idx_ready, 1)
                assert done[0] == STEPS

            def out_statistics(c):
                dve.wait_ge(out_copied, c + 3)
                nc.vector.bn_stats(ost[:, bass.ds(c, 1), :].rearrange("p a n -> p (a n)"), o[:, bass.ds(c * CP, CP)]).then_inc(bn_terms, 1)

            def chunk(c, parity, next_j, drain, ahead, prep=None):
                for k in range(TAPS):
                    dve.wait_ge(gathered[k], c * (16 * TILES) + 16 * TILES)
                    for q in range(1, 4):
                        for t in range(TILES):
                            if q == 1:
                                dve.wait_ge(scaled, c * (TAPS * TILES) + (TAPS * TILES + k * TILES + t + 1))
                            else:
                                dve.wait_ge(lerped, c * (TAPS * LERPS) + (TAPS * LERPS + k * LERPS + (q - 2) * TILES + t + 1))
                            a = acc[:, k % 3, t, :]
                            nc.vector.scalar_tensor_tensor(a, g[:, k, t, q, :], wt[:, parity, q, t, k:k + 1], a,
                                                           ALU.mult, ALU.add).then_inc(lerped, 1)
                    if drain and k == 2:
                        out_statistics(c - 1)
                    if ahead and k == 4:
                        indices(c + 1, next_j, 1 - parity)
                    if prep is not None:
                        prepare(*prep, k)

            dve.wait_ge(x0a_in, 16)
            statistics(0)
            group_norm(0, 0, ST0)
            dve.wait_ge(consts, 11)
            norm_xt(0)
            dve.wait_ge(gr_in, 16)
            indices(0, 0, 0)
            dve.wait_ge(granted, 1)
            chunk(0, 0, 1, False, True)
            with dve.Fori(0, B - 1) as b:
                for j in range(1, CHUNKS + 1):
                    chunk(b * CHUNKS + j, j % 2, (j + 1) % CHUNKS, True, True, (b + 1, j))
            with dve.Fori(0, PAIRS - 1) as i:
                chunk(2 * i + ((B - 1) * CHUNKS + 1), 1, 2 * i + 2, True, True)
                chunk(2 * i + ((B - 1) * CHUNKS + 2), 0, 2 * i + 3, True, True)
            dve.wait_ge(w1_in, 16)
            nc.vector.tensor_scalar(w_outer, w1_rows[:, :, 0], 0.5, None, ALU.mult).then_inc(w_mixed, 1)
            dve.wait_ge(w_mixed, 1)
            nc.vector.scalar_tensor_tensor(w_outer, w1_rows[:, :, 2], 0.5, w_outer, ALU.mult, ALU.add).then_inc(w_mixed, 1)
            dve.wait_ge(w_mixed, 2)
            nc.vector.scalar_tensor_tensor(w_plus, w1_rows[:, :, 1], 0.5, w_outer, ALU.mult, ALU.add).then_inc(w_mixed, 1)
            nc.vector.scalar_tensor_tensor(w_minus, w1_rows[:, :, 1], -0.5, w_outer, ALU.mult, ALU.add).then_inc(w_mixed, 1)
            chunk(ALL - 1, 1, None, True, False)
            out_statistics(ALL - 1)

            dve.wait_ge(bn_terms, ALL)
            dve.wait_ge(wc_in, 32)
            nc.vector.bn_aggr(omv[:], ost[:].rearrange("p a b -> p (a b)")).then_inc(bn_terms, 1)
            dve.wait_ge(bn_terms, ALL + 1)
            rsqrt(B, bna[:, 2:3], omv[:, 1:2])
            dve.wait_ge(rsqrt_step, (B + 1) * RSTEPS)
            nc.vector.tensor_tensor(bna[:, 0:1], bna[:, 2:3], params[:, 1:2], ALU.mult).then_inc(bn_terms, 1)
            dve.wait_ge(bn_terms, ALL + 2)
            nc.vector.tensor_tensor(bna[:, 2:3], omv[:, 0:1], bna[:, 0:1], ALU.mult).then_inc(bn_terms, 1)
            dve.wait_ge(bn_terms, ALL + 3)
            nc.vector.tensor_tensor(bna[:, 1:2], params[:, 2:3], bna[:, 2:3], ALU.subtract).then_inc(bn_ready, 1)

            def sums(b):
                def pieces(j):
                    alone(dve)
                    for i in range(2):
                        nc.vector.bn_stats(bst[:, 2 * j + i, :], x[:, bass.ds(b * HW + j * BP + i * HB, HB)]).then_inc(stats_in, 1)

                for j in range(1, BANDS, 2):
                    dve.wait_ge(relued, b * BANDS + (BAND_ORDER.index(j) + 1))
                    add_band(nc.vector, b, j).then_inc(summed, 1)
                    dve.wait_ge(summed, b * (BANDS // 2) + (j // 2 + 1))
                    pieces(j)
                for j in range(0, BANDS, 2):
                    dve.wait_ge(added, b * (BANDS // 2) + (j // 2 + 1))
                    pieces(j)
                aggregate(b * (2 * BANDS) + (B * CHUNKS + 2 * BANDS), 2 * BANDS)

            def finish(n, h):
                pairs = x[:, bass.ds(n * BP, BP)].rearrange("p (i two) -> p i two", two=2)
                even, odd = pairs[:, :, 0], pairs[:, :, 1]
                m0, m1, m2, m3 = (t[:, 0:HB] for t in MX[h % 2])
                s = n * 4
                dve.wait_ge(conv1, MIX * n + (2 + MIX * BANDS))
                nc.vector.scalar_tensor_tensor(even, m1, params[:, 3:4], even, ALU.add, ALU.add).then_inc(unmixed, 1)
                nc.vector.scalar_tensor_tensor(odd, m1, params[:, 3:4], odd, ALU.add, ALU.add).then_inc(unmixed, 1)
                dve.wait_ge(unmixed, s + 1)
                nc.vector.tensor_tensor(even, even, m0, ALU.add).then_inc(unmixed, 1)
                dve.wait_ge(conv1, MIX * n + (3 + MIX * BANDS))
                dve.wait_ge(unmixed, s + 2)
                nc.vector.tensor_tensor(odd, odd, m2, ALU.subtract).then_inc(unmixed, 1)
                dve.wait_ge(unmixed, s + 3)
                nc.vector.tensor_tensor(even, even, m2, ALU.add).then_inc(finished, 1)
                dve.wait_ge(conv1, MIX * n + (4 + MIX * BANDS))
                dve.wait_ge(unmixed, s + 4)
                nc.vector.tensor_tensor(odd, odd, m3, ALU.subtract).then_inc(finished, 1)

            sums(0)
            group_norm(B, B + 1, ST1)
            dve.wait_ge(normed, 1)
            for m in range(MIX):
                mix(nc.vector, 0, 0, m).then_inc(mixed0, 1)
            with dve.Fori(0, B - 1) as b:
                finish(b * BANDS, 0)
                sums(b + 1)
                finish(b * BANDS + 1, 1)
                group_norm(b + (B + 1), b + (B + 2), ST1)
                finish(b * BANDS + 2, 2)
                finish(b * BANDS + 3, 3)
            for h in range(BANDS):
                finish((B - 1) * BANDS + h, h)


def kernel(x, L0_conv_w_offset, L0_conv_b_offset, L0_conv_w_conv, L0_conv_b_conv, L0_conv_gamma, L0_conv_beta,
           L1_conv_weight, L1_conv_bias):
    import numpy as np
    import concourse.bacc as bacc
    from concourse.bass_utils import run_bass_kernel_spmd as run

    def taps_first(w):
        return np.ascontiguousarray(np.transpose(w, (1, 2, 3, 0))).reshape(P, TAPS, w.shape[0])

    order = [2 * k for k in range(9)] + [2 * k + 1 for k in range(9)] + list(range(18, 27))
    n = np.arange(HW).reshape(CHUNKS * TILES, P).T
    k = np.arange(TAPS)
    gy = (n // W)[:, :, None] + (k // 3 - 1)[None, None, :]
    gx = (n % W)[:, :, None] + (k % 3 - 1)[None, None, :]
    grid = np.concatenate([gy, gx], axis=2).astype(np.float32).reshape(P, CHUNKS, TILES, 18)
    arrays = {
        "x_dram": np.ascontiguousarray(np.transpose(np.asarray(x), (1, 0, 2, 3))).reshape(P, B, HW),
        "woff_dram": taps_first(np.asarray(L0_conv_w_offset)[order]),
        "wconv_dram": taps_first(np.asarray(L0_conv_w_conv)),
        "w1_dram": taps_first(np.asarray(L1_conv_weight)),
        "boff_dram": np.ascontiguousarray(np.asarray(L0_conv_b_offset)[order]).reshape(27, 1),
        "par_dram": np.ascontiguousarray(np.stack([np.asarray(v) for v in (
            L0_conv_b_conv, L0_conv_gamma, L0_conv_beta, L1_conv_bias)], axis=1)),
        "grid_dram": grid,
    }
    nc = bacc.Bacc("TRN2", target_bir_lowering=False, num_devices=1)
    aps = [nc.dram_tensor(name, a.shape, F32, kind="ExternalInput").ap() for name, a in arrays.items()]
    out = nc.dram_tensor("out_dram", (P, B * HW), F32, kind="ExternalOutput").ap()
    build(nc, *aps, out)
    r = run(nc, [arrays], core_ids=[0])
    y = r.results[0]["out_dram"].reshape(P, B, H, W)
    return np.ascontiguousarray(np.transpose(y, (1, 0, 2, 3)))
```
